# Optimizing a Trainium2 kernel written in Bass

```python
import numpy as np
import jax
import jax.numpy as jnp

def _softmax(x, axis=-1):
    return jax.nn.softmax(x, axis=axis)

def _gelu(x):
    return jax.nn.gelu(x, approximate=True)

def _silu(x):
    return jax.nn.silu(x)

def _sigmoid(x):
    return jax.nn.sigmoid(x)

def _layernorm(x, axis=-1, eps=1e-05):
    m = jnp.mean(x, axis=axis, keepdims=True)
    v = jnp.var(x, axis=axis, keepdims=True)
    return (x - m) / jnp.sqrt(v + eps)

def _scatter_add(tgt, idx, src, axis=0):
    return tgt.at[idx].add(src)

def _segment_sum(src, seg, n):
    return jax.ops.segment_sum(src, seg, n)
kernel_name = 'mk_sandwich_d1_jaxref_r8_58ec70'

def setup_inputs(seed: int=0):
    np.random.seed(seed)
    _w = jnp.asarray

    def _L0_attn_setup():
        import jax, jax.numpy as jnp
        import numpy as np
        EPS = 1e-05

        def xpos_rotate(x, offset=0, conjugate=False):
            b, s, h, dh = x.shape
            expoent = jnp.arange(0, dh, 2, dtype=jnp.float32) / dh
            angle = 10.0 ** (-4.0 * expoent)
            if conjugate:
                angle = -angle
            pos = jnp.arange(offset, s + offset, dtype=jnp.float32)
            nangle = pos[:, None] * angle[None, :]
            sin = jnp.sin(nangle)[None, :, None, :]
            cos = jnp.cos(nangle)[None, :, None, :]
            x0 = x[..., 0::2]
            x1 = x[..., 1::2]
            rot = jnp.stack([x0 * cos - x1 * sin, x0 * sin + x1 * cos], axis=-1)
            return rot.reshape(b, s, h, dh)

        def decay_mask(nseq, scale):
            idx = jnp.arange(nseq)
            diff = idx[:, None] - idx[None, :]
            mask = (diff >= 0).astype(scale.dtype)
            diff_c = jnp.maximum(diff, 0).astype(scale.dtype)
            logd = diff_c[None, :, :] * jnp.log(scale)[:, None, None]
            return jnp.exp(logd) * mask[None, :, :]

        def group_norm(R, gamma, beta, nheads):
            b, s, d = R.shape
            dh = d // nheads
            Rg = R.reshape(b, s, nheads, dh)
            mu = jnp.mean(Rg, axis=-1, keepdims=True)
            var = jnp.var(Rg, axis=-1, keepdims=True)
            Rn = (Rg - mu) * jax.lax.rsqrt(var + EPS)
            Rn = Rn * gamma.reshape(1, 1, nheads, dh) + beta.reshape(1, 1, nheads, dh)
            return Rn.reshape(b, s, d)
        key = jax.random.key(seed)
        ks = jax.random.split(key, 7)
        b, s, d, h = (2, 256, 128, 16)
        dh = d // h
        x = jax.random.normal(ks[0], (b, s, d), dtype=jnp.float32)
        std_qkv = float(np.sqrt(2.0 / (dh + d)))
        std_o = float(np.sqrt(2.0 / (d + d)))
        WQ = jax.random.normal(ks[1], (h, dh, d), dtype=jnp.float32) * std_qkv
        WK = jax.random.normal(ks[2], (h, dh, d), dtype=jnp.float32) * std_qkv
        WV = jax.random.normal(ks[3], (h, dh, d), dtype=jnp.float32) * std_qkv
        WO = jax.random.normal(ks[4], (d, d), dtype=jnp.float32) * std_o
        gamma = jnp.ones((d,), dtype=jnp.float32)
        beta = jnp.zeros((d,), dtype=jnp.float32)
        return {'x': x, 'WQ': WQ, 'WK': WK, 'WV': WV, 'WO': WO, 'gamma': gamma, 'beta': beta}
    _L0_attn_in = _L0_attn_setup()

    def _L0_ffn_setup():
        import jax, jax.numpy as jnp
        import numpy as np
        DIM = 128
        EXPERT_DIM = 64
        N_EXPERTS = 16
        TOPK = 2
        SHARED_HIDDEN = EXPERT_DIM * TOPK
        B, T = (4, 128)

        def _moe_forward(x, router_w, router_bias, up_proj, gate_proj, down_proj, sh_gate, sh_up, sh_down):
            Bb, Tt, D = x.shape
            flat = x.reshape(Bb * Tt, D)
            N = flat.shape[0]
            logits = flat @ router_w.T
            topk_scores, topk_idx = jax.lax.top_k(logits + router_bias, TOPK)
            topk_scores = jax.nn.softmax(topk_scores, axis=-1)
            combine = jnp.zeros((N, N_EXPERTS), flat.dtype)
            combine = combine.at[jnp.arange(N)[:, None], topk_idx].add(topk_scores)
            up_all = jnp.einsum('nd,kde->nke', flat, up_proj)
            gate_all = jnp.einsum('nd,kde->nke', flat, gate_proj)
            hidden = jax.nn.silu(gate_all) * up_all
            down_all = jnp.einsum('nke,ked->nkd', hidden, down_proj)
            out = jnp.einsum('nk,nkd->nd', combine, down_all)
            sh_hidden = jax.nn.silu(flat @ sh_gate.T) * (flat @ sh_up.T)
            out = out + sh_hidden @ sh_down.T
            return out.reshape(Bb, Tt, D)
        key = jax.random.key(seed)
        ks = jax.random.split(key, 9)
        std = 0.02
        return {'x': jax.random.normal(ks[0], (B, T, DIM), jnp.float32), 'router_w': jax.random.normal(ks[1], (N_EXPERTS, DIM), jnp.float32) * std, 'router_bias': jnp.zeros((N_EXPERTS,), jnp.float32), 'up_proj': jax.random.normal(ks[2], (N_EXPERTS, DIM, EXPERT_DIM), jnp.float32) * std, 'gate_proj': jax.random.normal(ks[3], (N_EXPERTS, DIM, EXPERT_DIM), jnp.float32) * std, 'down_proj': jax.random.normal(ks[4], (N_EXPERTS, EXPERT_DIM, DIM), jnp.float32) * std, 'sh_gate': jax.random.normal(ks[5], (SHARED_HIDDEN, DIM), jnp.float32) * std, 'sh_up': jax.random.normal(ks[6], (SHARED_HIDDEN, DIM), jnp.float32) * std, 'sh_down': jax.random.normal(ks[7], (DIM, SHARED_HIDDEN), jnp.float32) * std}
    _L0_ffn_in = _L0_ffn_setup()
    _d = {'L0_attn_x': _L0_attn_in['x'], 'L0_attn_WQ': _L0_attn_in['WQ'], 'L0_attn_WK': _L0_attn_in['WK'], 'L0_attn_WV': _L0_attn_in['WV'], 'L0_attn_WO': _L0_attn_in['WO'], 'L0_attn_gamma': _L0_attn_in['gamma'], 'L0_attn_beta': _L0_attn_in['beta'], 'L0_ffn_router_w': _L0_ffn_in['router_w'], 'L0_ffn_router_bias': _L0_ffn_in['router_bias'], 'L0_ffn_up_proj': _L0_ffn_in['up_proj'], 'L0_ffn_gate_proj': _L0_ffn_in['gate_proj'], 'L0_ffn_down_proj': _L0_ffn_in['down_proj'], 'L0_ffn_sh_gate': _L0_ffn_in['sh_gate'], 'L0_ffn_sh_up': _L0_ffn_in['sh_up'], 'L0_ffn_sh_down': _L0_ffn_in['sh_down']}
    _x0 = _d['L0_attn_x']
    _d['L0_attn_x'] = jax.random.normal(jax.random.fold_in(jax.random.key(seed), 1), (16, 256, 128), dtype=_x0.dtype)
    del _x0
    return _d

def reference(L0_attn_x, L0_attn_WQ, L0_attn_WK, L0_attn_WV, L0_attn_WO, L0_attn_gamma, L0_attn_beta, L0_ffn_router_w, L0_ffn_router_bias, L0_ffn_up_proj, L0_ffn_gate_proj, L0_ffn_down_proj, L0_ffn_sh_gate, L0_ffn_sh_up, L0_ffn_sh_down):

    def _L0_attn_ref(x, WQ, WK, WV, WO, gamma, beta):
        import jax, jax.numpy as jnp
        import numpy as np
        EPS = 1e-05

        def xpos_rotate(x, offset=0, conjugate=False):
            b, s, h, dh = x.shape
            expoent = jnp.arange(0, dh, 2, dtype=jnp.float32) / dh
            angle = 10.0 ** (-4.0 * expoent)
            if conjugate:
                angle = -angle
            pos = jnp.arange(offset, s + offset, dtype=jnp.float32)
            nangle = pos[:, None] * angle[None, :]
            sin = jnp.sin(nangle)[None, :, None, :]
            cos = jnp.cos(nangle)[None, :, None, :]
            x0 = x[..., 0::2]
            x1 = x[..., 1::2]
            rot = jnp.stack([x0 * cos - x1 * sin, x0 * sin + x1 * cos], axis=-1)
            return rot.reshape(b, s, h, dh)

        def decay_mask(nseq, scale):
            idx = jnp.arange(nseq)
            diff = idx[:, None] - idx[None, :]
            mask = (diff >= 0).astype(scale.dtype)
            diff_c = jnp.maximum(diff, 0).astype(scale.dtype)
            logd = diff_c[None, :, :] * jnp.log(scale)[:, None, None]
            return jnp.exp(logd) * mask[None, :, :]

        def group_norm(R, gamma, beta, nheads):
            b, s, d = R.shape
            dh = d // nheads
            Rg = R.reshape(b, s, nheads, dh)
            mu = jnp.mean(Rg, axis=-1, keepdims=True)
            var = jnp.var(Rg, axis=-1, keepdims=True)
            Rn = (Rg - mu) * jax.lax.rsqrt(var + EPS)
            Rn = Rn * gamma.reshape(1, 1, nheads, dh) + beta.reshape(1, 1, nheads, dh)
            return Rn.reshape(b, s, d)
        b, s, d = x.shape
        h, dh, _ = WQ.shape
        Q = jnp.einsum('bsd,hud->bshu', x, WQ)
        K = jnp.einsum('bsd,hud->bshu', x, WK)
        V = jnp.einsum('bsd,hud->bshu', x, WV)
        Q = xpos_rotate(Q)
        K = xpos_rotate(K)
        QK = jnp.einsum('bihd,bjhd->bhij', Q, K)
        scale = 1.0 - 2.0 ** (-5.0 - jnp.arange(h, dtype=jnp.float32))
        D = decay_mask(s, scale)
        QKD = QK * D[None]
        R = jnp.einsum('bhij,bjhd->bihd', QKD, V)
        R = R.reshape(b, s, d)
        R = group_norm(R, gamma, beta, h)
        y = R @ WO
        return y

    def _L0_ffn_ref(x, router_w, router_bias, up_proj, gate_proj, down_proj, sh_gate, sh_up, sh_down):
        import jax, jax.numpy as jnp
        import numpy as np
        DIM = 128
        EXPERT_DIM = 64
        N_EXPERTS = 16
        TOPK = 2
        SHARED_HIDDEN = EXPERT_DIM * TOPK
        B, T = (4, 128)

        def _moe_forward(x, router_w, router_bias, up_proj, gate_proj, down_proj, sh_gate, sh_up, sh_down):
            Bb, Tt, D = x.shape
            flat = x.reshape(Bb * Tt, D)
            N = flat.shape[0]
            logits = flat @ router_w.T
            topk_scores, topk_idx = jax.lax.top_k(logits + router_bias, TOPK)
            topk_scores = jax.nn.softmax(topk_scores, axis=-1)
            combine = jnp.zeros((N, N_EXPERTS), flat.dtype)
            combine = combine.at[jnp.arange(N)[:, None], topk_idx].add(topk_scores)
            up_all = jnp.einsum('nd,kde->nke', flat, up_proj)
            gate_all = jnp.einsum('nd,kde->nke', flat, gate_proj)
            hidden = jax.nn.silu(gate_all) * up_all
            down_all = jnp.einsum('nke,ked->nkd', hidden, down_proj)
            out = jnp.einsum('nk,nkd->nd', combine, down_all)
            sh_hidden = jax.nn.silu(flat @ sh_gate.T) * (flat @ sh_up.T)
            out = out + sh_hidden @ sh_down.T
            return out.reshape(Bb, Tt, D)
        return _moe_forward(x, router_w, router_bias, up_proj, gate_proj, down_proj, sh_gate, sh_up, sh_down)
    x = L0_attn_x
    x = x + _layernorm(_L0_attn_ref(_layernorm(x, axis=-1), L0_attn_WQ, L0_attn_WK, L0_attn_WV, L0_attn_WO, L0_attn_gamma, L0_attn_beta), axis=-1)
    x = x + _layernorm(_L0_ffn_ref(_layernorm(x, axis=-1), L0_ffn_router_w, L0_ffn_router_bias, L0_ffn_up_proj, L0_ffn_gate_proj, L0_ffn_down_proj, L0_ffn_sh_gate, L0_ffn_sh_up, L0_ffn_sh_down), axis=-1)
    return x

_drawn_inputs = setup_inputs


def setup_inputs(seed=0):
    import zlib

    import numpy as np

    out = dict(_drawn_inputs(seed))
    spreads = {'L0_attn_gamma': (1.0, 0.2), 'L0_attn_beta': (0.0, 0.1), 'L0_ffn_router_bias': (0.0, 0.1)}
    factors = {}
    for name, (base, spread) in spreads.items():
        noise = np.random.default_rng([zlib.crc32(name.encode()), seed]).standard_normal(out[name].shape)
        drawn = base * np.exp(spread * noise) if base else spread * noise
        out[name] = jnp.asarray(drawn.astype(out[name].dtype))
    for name, factor in factors.items():
        out[name] = (out[name] * factor).astype(out[name].dtype)
    return out
```

```python
import numpy as np
import concourse.bass as bass
from concourse import mybir
from concourse.alu_op_type import AluOpType as ALU
from contextlib import ExitStack

B, S, D, H = 16, 256, 128, 16
DH = D // H
E, F = 16, 64
P = 128
NB = 2
G = B // NB
R = S // P
T = NB * R
N = T * P
UNITS = E * F // P + 1
PAIRS = UNITS - 1
EPS = 1e-5
KV = H * DH * DH


def constants():
    pos = np.arange(S, dtype=np.float32)
    expo = np.arange(0, DH, 2, dtype=np.float32) / np.float32(DH)
    angle = (np.float32(10.0) ** (np.float32(-4.0) * expo)).astype(np.float32)
    turn = (pos[:, None] * angle[None, :]).astype(np.float32).astype(np.float64)
    cos, sin = np.cos(turn), np.sin(turn)
    scale = (1.0 - 2.0 ** (-5.0 - np.arange(H))).astype(np.float64)
    grow = scale[None, :] ** (np.arange(S)[:, None] - S // 2)
    cq = np.zeros((S, 2, H, DH))
    sq = np.zeros((S, 2, H, DH))
    for n, w in enumerate((grow, 1.0 / grow)):
        cq[:, n, :, 0::2] = cos[:, None, :] * w[:, :, None]
        cq[:, n, :, 1::2] = cos[:, None, :] * w[:, :, None]
        sq[:, n, :, 0::2] = -sin[:, None, :] * w[:, :, None]
        sq[:, n, :, 1::2] = sin[:, None, :] * w[:, :, None]
    cq = cq.reshape(P, R * 2 * D)
    sq = sq.reshape(P, R * 2 * D)
    before = np.triu(np.ones((P, P)), 1)
    ident = np.eye(P)
    count = np.broadcast_to(np.arange(E), (P, E))
    sel = np.zeros((P, PAIRS, P))
    for r in range(2 * E):
        for m in range(P):
            if (r % E) // 2 < PAIRS and (r % E) % 2 == m // F:
                sel[r, (r % E) // 2, m] = 1.0
    parts = [cq, sq, before, ident, count, sel.reshape(P, PAIRS * P)]
    return np.concatenate(parts, axis=1).astype(np.float32)


CC = [0]
for _w in (R * 2 * D, R * 2 * D, P, P, E, PAIRS * P):
    CC.append(CC[-1] + _w)


def build(nc, x, WQ, WK, WV, WO, gamma, beta, router_w, router_bias, up_proj, gate_proj,
          down_proj, sh_gate, sh_up, sh_down, consts, out):
    fp32 = mybir.dt.float32
    f32r = mybir.dt.float32r
    u32 = mybir.dt.uint32
    ACT = mybir.ActivationFunctionType
    AX = mybir.AxisListType.X

    with ExitStack() as ctx:
        def sb(name, shape, dt=fp32):
            return ctx.enter_context(nc.sbuf_tensor(name, shape, dt))

        def pb(name, width=512):
            return ctx.enter_context(nc.psum_tensor(name, [P, width], fp32))

        def sem(name):
            return ctx.enter_context(nc.semaphore(name))

        cst = sb("cst", [P, CC[-1]])
        rot_c = cst[:, CC[0]:CC[1]].rearrange("p (r n) -> p r n", r=R)
        rot_s = cst[:, CC[1]:CC[2]].rearrange("p (r n) -> p r n", r=R)
        before = cst[:, CC[2]:CC[3]]
        ident = cst[:, CC[3]:CC[4]]
        count = cst[:, CC[4]:CC[5]]
        sel_in = cst[0:2 * E, CC[5]:CC[6]]
        sel = sb("sel", [2 * E, PAIRS * P], f32r)
        w_in = sb("w_in", [P, 7, P])
        g_in = sb("g_in", [P, E * F])
        u_in = sb("u_in", [P, E * F])
        wqkv = sb("wqkv", [P, 3 * D])
        wo = sb("wo", [P, D])
        w_gate = [sb(f"w_gate{i}", [P, UNITS * P], f32r) for i in range(2)]
        w_up = [sb(f"w_up{i}", [P, UNITS * P], f32r) for i in range(2)]
        w_rout = [sb(f"w_rout{i}", [P, P], f32r) for i in range(2)]
        w_down = sb("w_down", [P, UNITS * D])
        gam = sb("gam", [P, 1])
        bet = sb("bet", [P, 1])
        rbias = sb("rbias", [E, 1])
        neghalf = sb("neghalf", [P, T * H])
        eps_t = sb("eps_t", [P, T * H])
        minus1 = sb("minus1", [P, T])

        x_ln = sb("x_ln", [P, T, D])
        x_res = sb("x_res", [P, T, D])
        ln1_s = sb("ln1_s", [P, T, 6])
        ln1_m = sb("ln1_m", [P, T, 2])
        ln1_r = sb("ln1_r", [P, T])
        xn = sb("xn", [P, T, D])
        xn_t = sb("xn_t", [P, N])
        qkv = sb("qkv", [P, NB, R, 3 * D])
        ra = sb("ra", [P, R, 2 * D])
        rb = sb("rb", [P, R, 2 * D])
        qk = sb("qk", [P, NB, R, 2 * D])
        kv_a = sb("kv_a", [P, KV])
        kv_b = sb("kv_b", [P, KV])
        kv_w = sb("kv_w", [P, KV])
        qs = sb("qs", [P, R, KV])
        ret = sb("ret", [P, NB, R, D])
        dp = sb("dp", [P, NB, R + 1, D])
        dots = sb("dots", [P, NB, (R + 1) * H])
        near = sb("near", [P, NB, R, D])
        near2 = sb("near2", [P, NB, D])
        ret_f = sb("ret_f", [P, T * D])
        gn_mu = sb("gn_mu", [P, T * H])
        ret_c = sb("ret_c", [P, T * D])
        gn_sq = sb("gn_sq", [P, T * D])
        gn_v = sb("gn_v", [P, T * H])
        gn_r = sb("gn_r", [P, T * H])
        ret_n = sb("ret_n", [P, T * D])
        ret_t = sb("ret_t", [P, N])
        y_s = sb("y_s", [P, T, 6])
        y_m = sb("y_m", [P, T, 2])
        y_r = sb("y_r", [P, T])
        y_b = sb("y_b", [P, T])
        y_n = sb("y_n", [P, T, D])
        x1 = [sb(f"x1_{i}", [P, T, D]) for i in range(2)]
        ln2_s = sb("ln2_s", [P, T, 6])
        ln2_m = sb("ln2_m", [P, T, 2])
        ln2_r = sb("ln2_r", [P, T])
        xm = sb("xm", [P, T, D])
        xm_hi = [sb(f"xm_hi{i}", [P, N], f32r) for i in range(2)]
        xm_lo = [sb(f"xm_lo{i}", [P, N], f32r) for i in range(2)]

        lg_t = sb("lg_t", [E, N])
        lg = sb("lg", [P, T, E])
        top = sb("top", [P, T, 8])
        idx = sb("idx", [P, T, 8], u32)
        idx_f = sb("idx_f", [P, T, 2])
        gap = sb("gap", [P, T])
        th = sb("th", [P, T])
        prob = sb("prob", [P, T, 2])
        hot = sb("hot", [P, T, 2, E])
        hot_p = sb("hot_p", [P, T, 2, E])
        comb = sb("comb", [P, T, E])
        comb_2 = sb("comb_2", [P, T, 2 * E], f32r)
        comb_t = [sb(f"comb_t{i}", [2 * E, N], f32r) for i in range(2)]

        sil = [sb(f"sil{i}", [P, N]) for i in range(2)]
        cbc = [sb(f"cbc{i}", [P, N]) for i in range(2)]
        silc = [sb(f"silc{i}", [P, N]) for i in range(2)]
        hid = [sb(f"hid{i}", [P, N]) for i in range(2)]
        y2_t = sb("y2_t", [P, N])
        y2_s = sb("y2_s", [P, T, 6])
        y2_m = sb("y2_m", [P, T, 2])
        y2_r = sb("y2_r", [P, T])
        y2_b = sb("y2_b", [P, T])
        y2_n = sb("y2_n", [P, T, D])
        x2 = sb("x2", [P, T, D])
        carrier = sb("carrier", [P, 1])

        ps_g = pb("ps_g")
        ps_u = pb("ps_u")
        ps_c = pb("ps_c")
        ps_y = pb("ps_y")
        ps_s = pb("ps_s", 1024)
        ps_ab = pb("ps_ab", 1024)
        ps_a, ps_b = ps_ab[:, 0:512], ps_ab[:, 512:1024]
        ps_t = ps_s[:, 512:1024]

        PER = {}

        def count_sem(name, per=1):
            s = sem(name)
            PER[name] = per
            return s

        names = dict(
            x_in=16, xres_in=16, ln1_st=1, ln1_mv=1, ln1_rs=2, xn_done=1, xnt_ps=1, xnt_sb=1,
            proj_ps=NB, qkv_sb=NB, rot_ab=NB, qk_done=NB, kv_ab=NB, kv_done=NB, pre_ps=NB, qs_done=NB,
            ret_done=NB, dp_done=NB, dots_done=NB, near_ab=NB, near_done=NB,
            retf_done=1, mu_done=1, retc_done=1, sq_done=1, gnv_done=1, gnr_done=2, retn_done=1,
            rett_ps=1, rett_sb=1, wo_ps=1, y_st=1, y_mv=1, y_rs=3, yn_done=1, x1_done=1,
            ln2_st=1, ln2_mv=1, ln2_rs=2, xm_done=1, xmt_ps=1, xmhi_done=1, xmlo_done=1,
            rout_ps=1, lgt_sb=1, lg_ps=1, lg_sb=1, top_done=1, idx_done=1, gap_done=1, th_done=1,
            prob_done=1, idxf_done=1, hot_done=1, hotp_done=1, comb_done=1, chi_done=1, clo_done=1,
            ct_ps=1, ct_sb=1,
            gate_ps=UNITS, up_ps=UNITS, c_ps=PAIRS, sil_done=UNITS, cbc_done=PAIRS, silc_done=PAIRS,
            hid_done=UNITS, down_ps=UNITS, y2t_sb=1, y2_ps=1, y2_st=1, y2_mv=1, y2_rs=3,
            y2n_done=1, x2_done=1, stored=16)
        sems = {k: count_sem(k, v) for k, v in names.items()}
        loaded = [sem(f"loaded{i}") for i in range(15)]
        wt_ps = sem("wt_ps")
        wt_sb = sem("wt_sb")
        w_ready = sem("w_ready")
        small_ready = sem("small_ready")

        def wait(eng, name, g, n=None):
            per = PER[name]
            n = per if n is None else n
            if isinstance(g, int):
                if g >= G:
                    g, n = G - 1, per
                if g * per + n > 0:
                    eng.wait_ge(sems[name], g * per + n)
            else:
                eng.wait_ge(sems[name], g * per + n)

        x_v = x.rearrange("n (p r) d -> p n (r d)", r=R)
        out_v = out.rearrange("n (p r) d -> p n (r d)", r=R)

        def batches(view, g):
            if isinstance(g, int):
                return view[:, NB * g:NB * g + NB, :]
            return view[:, bass.ds(NB * g, NB), :]

        def tb(t):
            return slice(t * P, t * P + P)

        def steps(eng, step):
            step(0, 0, True, False, False)
            step(1, 1, True, True, False)
            with eng.Fori(1, G // 2) as i:
                step(i * 2, 0, True, True, True)
                step(i * 2 + 1, 1, True, True, True)
            step(G, G % 2, False, True, True)
            step(G + 1, (G + 1) % 2, False, False, True)

        block = ctx.enter_context(nc.Block())

        @block.sync
        def _(sp):
            sp.dma_start(cst[:, :], consts).then_inc(loaded[0], 16)
            for i, w in enumerate((WQ, WK, WV)):
                sp.dma_start(w_in[:, i, :], w.rearrange("h u d -> (h u) d")).then_inc(loaded[1 + i], 16)
            sp.dma_start(wo[:, :], WO).then_inc(loaded[4], 16)
            sp.dma_start(g_in[:, :].rearrange("p (e f) -> p e f", f=F),
                         gate_proj.rearrange("e d f -> d e f")).then_inc(loaded[5], 16)
            sp.dma_start(u_in[:, :].rearrange("p (e f) -> p e f", f=F),
                         up_proj.rearrange("e d f -> d e f")).then_inc(loaded[6], 16)
            sp.dma_start(w_in[:, 3, :], sh_gate).then_inc(loaded[7], 16)
            sp.dma_start(w_in[:, 4, :], sh_up).then_inc(loaded[8], 16)
            sp.dma_start(w_in[:, 5, :], sh_down).then_inc(loaded[9], 16)
            sp.wait_ge(small_ready, 1)
            sp.dma_start(w_in[0:E, 6, :], router_w).then_inc(loaded[10], 16)
            sp.dma_start(w_down[:, 0:PAIRS * D].rearrange("p (e d) -> p e d", d=D),
                         down_proj.rearrange("(n e) f d -> (e f) n d", e=2)).then_inc(loaded[11], 16)

            def step(s, q, att, moe, tail):
                if att:
                    wait(sp, "xn_done", s - 1)
                    sp.dma_start(x_ln[:, :, :].rearrange("p (n r) d -> p n (r d)", r=R),
                                 batches(x_v, s)).then_inc(sems["x_in"], 16)
                    wait(sp, "x1_done", s - 1)
                    sp.dma_start(x_res[:, :, :].rearrange("p (n r) d -> p n (r d)", r=R),
                                 batches(x_v, s)).then_inc(sems["xres_in"], 16)
                if tail:
                    wait(sp, "x2_done", s - 2)
                    sp.dma_start(batches(out_v, s - 2),
                                 x2[:, :, :].rearrange("p (n r) d -> p n (r d)", r=R)
                                 ).then_inc(sems["stored"], 16)

            steps(sp, step)
            sp.wait_ge(sems["stored"], 16 * G)

        @block.gpsimd
        def _(pool):
            nc.gpsimd.memset(w_in[:, 6, :], 0.0).then_inc(small_ready, 1)
            nc.gpsimd.memset(eps_t[:, :], EPS)
            nc.gpsimd.memset(minus1[:, :], -1.0)
            nc.gpsimd.memset(neghalf[:, :], -0.5).then_inc(small_ready, 1)
            pool.dma_start(gam[:, :], gamma.rearrange("(p a) -> p a", a=1)).then_inc(loaded[12], 16)
            pool.dma_start(bet[:, :], beta.rearrange("(p a) -> p a", a=1)).then_inc(loaded[13], 16)
            pool.dma_start(rbias[:, :], router_bias.rearrange("(p a) -> p a", a=1)).then_inc(loaded[14], 16)
            pool.wait_ge(small_ready, 2)

            def rstd(name, g, dst, var):
                n = dst.free_size()
                nc.gpsimd.tensor_tensor(dst, var, eps_t[:, 0:n], ALU.add).then_inc(sems[name], 1)
                wait(pool, name, g, 1)
                nc.gpsimd.tensor_tensor(dst, dst, neghalf[:, 0:n], ALU.pow).then_inc(sems[name], 1)

            def rstd_bias(name, g, r, bias, mv):
                nc.gpsimd.tensor_tensor(bias, mv[:, :, 0], minus1[:, :], ALU.mult)
                rstd(name, g, r, mv[:, :, 1])
                wait(pool, name, g, 2)
                nc.gpsimd.tensor_tensor(bias, bias, r, ALU.mult).then_inc(sems[name], 1)

            def outer(b, r, dst):
                k = qk[:, b, r, D:2 * D].rearrange("p (h u) -> p h u", u=DH)
                v = qkv[:, b, r, 2 * D:3 * D].rearrange("p (h v) -> p h v", v=DH)
                return nc.gpsimd.tensor_tensor(
                    dst[:, :].rearrange("p (h u v) -> p h u v", u=DH, v=DH),
                    k.unsqueeze(3).broadcast_to([P, H, DH, DH]),
                    v.unsqueeze(2).broadcast_to([P, H, DH, DH]), ALU.mult)

            def step(s, q, att, moe, tail):
                def experts(k):
                    if k == PAIRS:
                        return
                    wait(pool, "sil_done", s - 1, k + 1)
                    wait(pool, "cbc_done", s - 1, k + 1)
                    if k >= 2:
                        wait(pool, "hid_done", s - 1, k - 1)
                    else:
                        wait(pool, "hid_done", s - 2, PAIRS - 1 + k)
                    nc.gpsimd.tensor_tensor(silc[k % 2][:, :], sil[k % 2][:, :], cbc[k % 2][:, :],
                                            ALU.mult).then_inc(sems["silc_done"], 1)

                for k in range(UNITS):
                    if att and k == 0:
                        wait(pool, "ln1_mv", s)
                        rstd("ln1_rs", s, ln1_r[:, :], ln1_m[:, :, 1])
                    if tail and k == 0:
                        wait(pool, "y2_mv", s - 2)
                        rstd_bias("y2_rs", s - 2, y2_r[:, :], y2_b[:, :], y2_m)
                    if moe:
                        experts(k)
                    if tail and k == 1:
                        wait(pool, "y2n_done", s - 2)
                        wait(pool, "stored", s - 3)
                        nc.gpsimd.tensor_tensor(x2[:, :, :], y2_n[:, :, :], x1[q][:, :, :],
                                                ALU.add).then_inc(sems["x2_done"], 1)
                    if att and k in (1, 2, 3, 4):
                        b = 0 if k < 3 else 1
                        if k in (1, 3):
                            wait(pool, "kv_done", s - 1 if b == 0 else s, NB if b == 0 else b)
                            wait(pool, "qk_done", s, b + 1)
                            outer(b, 0, kv_a)
                            outer(b, 1, kv_b).then_inc(sems["kv_ab"], 1)
                        else:
                            wait(pool, "kv_ab", s, b + 1)
                            wait(pool, "pre_ps", s - 1 if b == 0 else s, NB if b == 0 else b)
                            nc.gpsimd.tensor_tensor(kv_w[:, :], kv_a[:, :], kv_b[:, :],
                                                    ALU.add).then_inc(sems["kv_done"], 1)
                    if att and k in (3, 5):
                        b = 0 if k == 3 else 1
                        near_terms(s, b)
                    if att and k == 6:
                        wait(pool, "gnv_done", s)
                        rstd("gnr_done", s, gn_r[:, :], gn_v[:, :])
                    if att and k == 7:
                        wait(pool, "y_mv", s)
                        rstd_bias("y_rs", s, y_r[:, :], y_b[:, :], y_m)
                        wait(pool, "yn_done", s)
                        wait(pool, "xres_in", s)
                        wait(pool, "x2_done", s - 2)
                        nc.gpsimd.tensor_tensor(x1[q][:, :, :], y_n[:, :, :], x_res[:, :, :],
                                                ALU.add).then_inc(sems["x1_done"], 1)
                        wait(pool, "ln2_mv", s)
                        rstd("ln2_rs", s, ln2_r[:, :], ln2_m[:, :, 1])

            def near_terms(s, b):
                wait(pool, "dots_done", s, b + 1)
                wait(pool, "retf_done", s - 1)
                d = dots[:, b, :].rearrange("p (n h) -> p n h", h=H)
                v = qkv[:, b, :, 2 * D:3 * D].rearrange("p r (h v) -> p r h v", v=DH)
                for r in range(R):
                    nc.gpsimd.tensor_tensor(near[:, b, r, :].rearrange("p (h v) -> p h v", v=DH),
                                            d[:, r, :].unsqueeze(2).broadcast_to([P, H, DH]),
                                            v[:, 0, :, :], ALU.mult)
                nc.gpsimd.tensor_tensor(near2[:, b, :].rearrange("p (h v) -> p h v", v=DH),
                                        d[:, R, :].unsqueeze(2).broadcast_to([P, H, DH]),
                                        v[:, 1, :, :], ALU.mult).then_inc(sems["near_ab"], 1)
                wait(pool, "near_ab", s, b + 1)
                nc.gpsimd.tensor_tensor(near[:, b, 1, :], near[:, b, 1, :], near2[:, b, :],
                                        ALU.add).then_inc(sems["near_done"], 1)

            steps(pool, step)

        @block.scalar
        def _(act):
            act.wait_ge(loaded[0], 16)
            nc.scalar.activation(sel[:, :], sel_in, ACT.Copy).then_inc(w_ready, 1)
            act.wait_ge(wt_ps, 1)
            nc.scalar.activation(wqkv[:, :], ps_g[:, 0:3 * D], ACT.Copy).then_inc(wt_sb, 1)
            act.wait_ge(loaded[5], 16)
            nc.scalar.activation(w_gate[0][:, 0:PAIRS * P], g_in[:, :], ACT.Copy).then_inc(w_ready, 1)
            act.wait_ge(loaded[6], 16)
            nc.scalar.activation(w_up[0][:, 0:PAIRS * P], u_in[:, :], ACT.Copy).then_inc(w_ready, 1)
            act.wait_ge(wt_ps, 2)
            nc.scalar.activation(w_gate[0][:, PAIRS * P:], ps_u[:, 0:P], ACT.Copy)
            nc.scalar.activation(w_up[0][:, PAIRS * P:], ps_u[:, P:2 * P], ACT.Copy)
            nc.scalar.activation(w_down[:, PAIRS * D:], ps_u[:, 2 * P:3 * P], ACT.Copy)
            nc.scalar.activation(w_rout[0][:, :], ps_u[:, 3 * P:4 * P], ACT.Copy).then_inc(w_ready, 1)
            for i in (12, 13, 14):
                act.wait_ge(loaded[i], 16)

            def step(s, q, att, moe, tail):
                for k in range(UNITS):
                    if tail and k == 0:
                        wait(act, "down_ps", s - 2)
                        wait(act, "y2_ps", s - 3)
                        nc.scalar.activation(y2_t[:, :], ps_y[:, :], ACT.Copy).then_inc(sems["y2t_sb"], 1)
                    if moe:
                        if k < PAIRS:
                            wait(act, "c_ps", s - 1, k + 1)
                            if k >= 2:
                                wait(act, "silc_done", s - 1, k - 1)
                            else:
                                wait(act, "silc_done", s - 2, PAIRS - 1 + k)
                            nc.scalar.activation(cbc[k % 2][:, :], ps_c[:, :],
                                                 ACT.Copy).then_inc(sems["cbc_done"], 1)
                        wait(act, "gate_ps", s - 1, k + 1)
                        if k >= 2:
                            wait(act, "silc_done", s - 1, k - 1)
                        elif k == 0:
                            wait(act, "hid_done", s - 2)
                        else:
                            wait(act, "silc_done", s - 2)
                        nc.scalar.activation(sil[k % 2][:, :], ps_g[:, :],
                                             ACT.Silu).then_inc(sems["sil_done"], 1)
                    if tail and k == 0:
                        wait(act, "y2_rs", s - 2)
                        wait(act, "x2_done", s - 3)
                        for t in range(T):
                            i = nc.scalar.activation(y2_n[:, t, :], ps_t[:, tb(t)], ACT.Identity,
                                                     bias=y2_b[:, t:t + 1], scale=y2_r[:, t:t + 1])
                        i.then_inc(sems["y2n_done"], 1)
                    if att and k == 0:
                        wait(act, "xnt_ps", s)
                        wait(act, "proj_ps", s - 1)
                        nc.scalar.activation(xn_t[:, :], ps_a, ACT.Copy).then_inc(sems["xnt_sb"], 1)
                    if att and k in (1, 2):
                        b = k - 1
                        wait(act, "proj_ps", s, b + 1)
                        wait(act, "near_done", s - 1, b + 1)
                        wait(act, "kv_ab", s - 1, b + 1)
                        nc.scalar.activation(
                            qkv[:, b, :, :], ps_ab[:, :].rearrange("p (r n) -> p r n", r=R)[:, :, 0:3 * D],
                            ACT.Copy).then_inc(sems["qkv_sb"], 1)
                    if att and k == 6:
                        wait(act, "retc_done", s)
                        wait(act, "gnv_done", s - 1)
                        nc.scalar.activation(gn_sq[:, :], ret_c[:, :], ACT.Square,
                                             scale=DH ** -0.5).then_inc(sems["sq_done"], 1)
                        wait(act, "rett_ps", s)
                        wait(act, "wo_ps", s - 1)
                        nc.scalar.activation(ret_t[:, :], ps_a, ACT.Identity, bias=bet[:, :],
                                             scale=gam[:, :]).then_inc(sems["rett_sb"], 1)
                    if att and k == 7:
                        wait(act, "y_rs", s)
                        wait(act, "x1_done", s - 1)
                        for t in range(T):
                            i = nc.scalar.activation(y_n[:, t, :], ps_b[:, tb(t)], ACT.Identity,
                                                     bias=y_b[:, t:t + 1], scale=y_r[:, t:t + 1])
                        i.then_inc(sems["yn_done"], 1)
                    if att and k == 8:
                        wait(act, "xmt_ps", s)
                        wait(act, "up_ps", s - 2)
                        wait(act, "gate_ps", s - 2)
                        nc.scalar.activation(xm_hi[q][:, :], ps_a, ACT.Copy).then_inc(sems["xmhi_done"], 1)
                        wait(act, "rout_ps", s)
                        nc.scalar.activation(lg_t[:, :], ps_b[0:E, :], ACT.Identity,
                                             bias=rbias[:, :]).then_inc(sems["lgt_sb"], 1)
                        wait(act, "gap_done", s)
                        nc.scalar.activation(th[:, :], gap[:, :], ACT.Tanh, scale=0.5).then_inc(sems["th_done"], 1)
                        wait(act, "ct_ps", s)
                        wait(act, "c_ps", s - 2)
                        nc.scalar.activation(comb_t[q][:, :], ps_b[0:2 * E, :],
                                             ACT.Copy).then_inc(sems["ct_sb"], 1)

            steps(act, step)

        @block.vector
        def _(dve):
            dve.wait_ge(w_ready, 2)
            nc.vector.tensor_tensor(w_gate[1][:, 0:PAIRS * P], g_in[:, :],
                                    w_gate[0][:, 0:PAIRS * P].bitcast(fp32), ALU.subtract)
            dve.wait_ge(w_ready, 3)
            nc.vector.tensor_tensor(w_up[1][:, 0:PAIRS * P], u_in[:, :],
                                    w_up[0][:, 0:PAIRS * P].bitcast(fp32), ALU.subtract)
            dve.wait_ge(w_ready, 4)
            nc.vector.tensor_tensor(w_gate[1][:, PAIRS * P:], ps_u[:, 0:P],
                                    w_gate[0][:, PAIRS * P:].bitcast(fp32), ALU.subtract)
            nc.vector.tensor_tensor(w_up[1][:, PAIRS * P:], ps_u[:, P:2 * P],
                                    w_up[0][:, PAIRS * P:].bitcast(fp32), ALU.subtract)
            nc.vector.tensor_tensor(w_rout[1][:, :], ps_u[:, 3 * P:4 * P],
                                    w_rout[0][:, :].bitcast(fp32), ALU.subtract).then_inc(w_ready, 1)

            def carry_wait():
                nc.vector.memset(carrier[:, :], 0.0)

            def stats(s, st, mv, sem_st, sem_mv, src):
                for t in range(T):
                    i = nc.vector.bn_stats(st[:, t, :], src(t))
                i.then_inc(sems[sem_st], 1)
                wait(dve, sem_st, s)
                carry_wait()
                for t in range(T):
                    i = nc.vector.bn_aggr(mv[:, t, :], st[:, t, :])
                i.then_inc(sems[sem_mv], 1)

            def rotate(s, b):
                wait(dve, "qkv_sb", s, b + 1)
                src = qkv[:, b, :, 0:2 * D]
                for r in range(R):
                    sw = src[:, r, :].rearrange("p (n c) -> p n c", c=2)[:, :, ::-1]
                    nc.vector.tensor_tensor(rb[:, r, :].rearrange("p (n c) -> p n c", c=2), sw,
                                            rot_s[:, r, :].rearrange("p (n c) -> p n c", c=2), ALU.mult)
                nc.vector.tensor_tensor(ra[:, :, :], src, rot_c, ALU.mult).then_inc(sems["rot_ab"], 1)
                wait(dve, "rot_ab", s, b + 1)
                wait(dve, "kv_ab", s - 1, b + 1)
                nc.vector.tensor_tensor(qk[:, b, :, :], ra[:, :, :], rb[:, :, :],
                                        ALU.add).then_inc(sems["qk_done"], 1)

            def near_dots(s, b):
                wait(dve, "dots_done", s - 1, b + 1)
                wait(dve, "qk_done", s, b + 1)
                nc.vector.tensor_tensor(dp[:, b, 0:R, :], qk[:, b, :, 0:D],
                                        qk[:, b, 0, D:2 * D].unsqueeze(1).broadcast_to([P, R, D]), ALU.mult)
                nc.vector.tensor_tensor(dp[:, b, R, :], qk[:, b, 1, 0:D], qk[:, b, 1, D:2 * D],
                                        ALU.mult).then_inc(sems["dp_done"], 1)
                wait(dve, "dp_done", s, b + 1)
                wait(dve, "near_ab", s - 1, b + 1)
                nc.vector.tensor_reduce(dots[:, b, :], dp[:, b, :, :].rearrange("p n (h u) -> p (n h) u", u=DH),
                                        AX, ALU.add).then_inc(sems["dots_done"], 1)

            def apply_q(s, b):
                wait(dve, "ret_done", s - 1 if b == 0 else s, NB if b == 0 else b)
                wait(dve, "pre_ps", s, b + 1)
                for r in range(R):
                    i = nc.vector.tensor_tensor(
                        qs[:, r, :].rearrange("p (n v) -> p n v", v=DH),
                        ps_s[:, :].rearrange("p (n v) -> p n v", v=DH),
                        qk[:, b, r, 0:D].unsqueeze(2).broadcast_to([P, D, DH]), ALU.mult)
                i.then_inc(sems["qs_done"], 1)

            def reduce_q(s, b):
                wait(dve, "qs_done", s, b + 1)
                for r in range(R):
                    i = nc.vector.tensor_reduce(ret[:, b, r, :].rearrange("p (h v) -> p h v", v=DH),
                                                qs[:, r, :].rearrange("p (h u v) -> p h v u", u=DH, v=DH),
                                                AX, ALU.add)
                i.then_inc(sems["ret_done"], 1)

            def experts(s, k):
                wait(dve, "up_ps", s - 1, k + 1)
                if k < PAIRS:
                    wait(dve, "silc_done", s - 1, k + 1)
                    other = silc[k % 2]
                else:
                    wait(dve, "sil_done", s - 1, k + 1)
                    other = sil[k % 2]
                if k >= 2:
                    wait(dve, "down_ps", s - 1, k - 1)
                else:
                    wait(dve, "down_ps", s - 2, UNITS - k)
                nc.vector.tensor_tensor(hid[k % 2][:, :], ps_u[:, :], other[:, :],
                                        ALU.mult).then_inc(sems["hid_done"], 1)

            def step(s, q, att, moe, tail):
                for k in range(UNITS):
                    if att and k == 0:
                        wait(dve, "x_in", s)
                        stats(s, ln1_s, ln1_m, "ln1_st", "ln1_mv", lambda t: x_ln[:, t, :])
                    if tail and k == 0:
                        wait(dve, "y2_ps", s - 2)
                        stats(s - 2, y2_s, y2_m, "y2_st", "y2_mv", lambda t: ps_t[:, tb(t)])
                    if att and k == 0:
                        wait(dve, "ln1_rs", s)
                        for t in range(T):
                            i = nc.vector.tensor_scalar(xn[:, t, :], x_ln[:, t, :], ln1_m[:, t, 0:1],
                                                        ln1_r[:, t:t + 1], ALU.subtract, ALU.mult)
                        i.then_inc(sems["xn_done"], 1)
                    if moe:
                        experts(s, k)
                    if att:
                        if k in (1, 2):
                            rotate(s, k - 1)
                            near_dots(s, k - 1)
                        elif k == 4:
                            apply_q(s, 0)
                        elif k == 5:
                            reduce_q(s, 0)
                            apply_q(s, 1)
                        elif k == 6:
                            reduce_q(s, 1)
                            group_norm(s)
                        elif k == 7:
                            out_norm(s, q)
                        elif k == 8:
                            routing(s, q)

            def group_norm(s):
                wait(dve, "near_done", s)
                wait(dve, "ret_done", s)
                nc.vector.tensor_tensor(ret_f[:, :], ret[:, :, :, :].rearrange("p n r d -> p (n r d)"),
                                        near[:, :, :, :].rearrange("p n r d -> p (n r d)"),
                                        ALU.add).then_inc(sems["retf_done"], 1)
                wait(dve, "retf_done", s)
                rf = ret_f[:, :].rearrange("p (n v) -> p n v", v=DH)
                nc.vector.tensor_reduce(gn_mu[:, :], rf, AX, ALU.add).then_inc(sems["mu_done"], 1)
                wait(dve, "mu_done", s)
                rc = ret_c[:, :].rearrange("p (n v) -> p n v", v=DH)
                nc.vector.scalar_tensor_tensor(rc, gn_mu[:, :].unsqueeze(2).broadcast_to([P, T * H, DH]),
                                               -1.0 / DH, rf, ALU.mult, ALU.add).then_inc(sems["retc_done"], 1)
                wait(dve, "sq_done", s)
                nc.vector.tensor_reduce(gn_v[:, :], gn_sq[:, :].rearrange("p (n v) -> p n v", v=DH),
                                        AX, ALU.add).then_inc(sems["gnv_done"], 1)
                wait(dve, "gnr_done", s)
                nc.vector.tensor_tensor(ret_n[:, :].rearrange("p (n v) -> p n v", v=DH), rc,
                                        gn_r[:, :].unsqueeze(2).broadcast_to([P, T * H, DH]),
                                        ALU.mult).then_inc(sems["retn_done"], 1)

            def out_norm(s, q):
                wait(dve, "wo_ps", s)
                stats(s, y_s, y_m, "y_st", "y_mv", lambda t: ps_b[:, tb(t)])
                wait(dve, "x1_done", s)
                stats(s, ln2_s, ln2_m, "ln2_st", "ln2_mv", lambda t: x1[q][:, t, :])
                wait(dve, "ln2_rs", s)
                for t in range(T):
                    i = nc.vector.tensor_scalar(xm[:, t, :], x1[q][:, t, :], ln2_m[:, t, 0:1],
                                                ln2_r[:, t:t + 1], ALU.subtract, ALU.mult)
                i.then_inc(sems["xm_done"], 1)

            def routing(s, q):
                wait(dve, "xmhi_done", s)
                nc.vector.tensor_tensor(xm_lo[q][:, :], ps_a, xm_hi[q][:, :].bitcast(fp32),
                                        ALU.subtract).then_inc(sems["xmlo_done"], 1)
                wait(dve, "lg_ps", s)
                nc.vector.tensor_copy(lg[:, :, :].rearrange("p t e -> p (t e)"),
                                      ps_a[:, 0:T * E]).then_inc(sems["lg_sb"], 1)
                wait(dve, "lg_sb", s)
                carry_wait()
                for t in range(T):
                    i = nc.vector.max(top[:, t, :], lg[:, t, :])
                i.then_inc(sems["top_done"], 1)
                wait(dve, "top_done", s)
                nc.vector.tensor_tensor(gap[:, :], top[:, :, 1], top[:, :, 0],
                                        ALU.subtract).then_inc(sems["gap_done"], 1)
                for t in range(T):
                    i = nc.vector.max_index(idx[:, t, :], top[:, t, :], lg[:, t, :])
                i.then_inc(sems["idx_done"], 1)
                wait(dve, "idx_done", s)
                nc.vector.tensor_copy(idx_f[:, :, :], idx[:, :, 0:2]).then_inc(sems["idxf_done"], 1)
                wait(dve, "idxf_done", s)
                nc.vector.tensor_tensor(hot[:, :, :, :].rearrange("p t c e -> p (t c) e"),
                                        count.unsqueeze(1).broadcast_to([P, 2 * T, E]),
                                        idx_f[:, :, :].rearrange("p t c -> p (t c)").unsqueeze(2)
                                        .broadcast_to([P, 2 * T, E]), ALU.is_equal).then_inc(sems["hot_done"], 1)
                wait(dve, "th_done", s)
                nc.vector.tensor_scalar(prob[:, :, 0], th[:, :], -0.5, 0.5, ALU.mult, ALU.add)
                nc.vector.tensor_scalar(prob[:, :, 1], th[:, :], 0.5, 0.5, ALU.mult,
                                        ALU.add).then_inc(sems["prob_done"], 1)
                wait(dve, "prob_done", s)
                wait(dve, "hot_done", s)
                nc.vector.tensor_tensor(hot_p[:, :, :, :].rearrange("p t c e -> p (t c) e"),
                                        hot[:, :, :, :].rearrange("p t c e -> p (t c) e"),
                                        prob[:, :, :].rearrange("p t c -> p (t c)").unsqueeze(2)
                                        .broadcast_to([P, 2 * T, E]), ALU.mult).then_inc(sems["hotp_done"], 1)
                wait(dve, "hotp_done", s)
                nc.vector.tensor_tensor(comb[:, :, :], hot_p[:, :, 0, :], hot_p[:, :, 1, :],
                                        ALU.add).then_inc(sems["comb_done"], 1)
                wait(dve, "comb_done", s)
                nc.vector.tensor_copy(comb_2[:, :, 0:E], comb[:, :, :]).then_inc(sems["chi_done"], 1)
                wait(dve, "chi_done", s)
                nc.vector.tensor_tensor(comb_2[:, :, E:2 * E], comb[:, :, :],
                                        comb_2[:, :, 0:E].bitcast(fp32),
                                        ALU.subtract).then_inc(sems["clo_done"], 1)

            steps(dve, step)

        @block.tensor
        def _(pe):
            mm = nc.tensor.matmul
            pe.wait_ge(loaded[0], 16)
            for i in range(3):
                pe.wait_ge(loaded[1 + i], 16)
                t_ = nc.tensor.transpose(ps_g[:, tb(i)], w_in[:, i, :], ident)
            t_.then_inc(wt_ps, 1)
            for i in range(4):
                pe.wait_ge(loaded[7 + i], 16)
                t_ = nc.tensor.transpose(ps_u[:, tb(i)], w_in[:, 3 + i, :], ident)
            t_.then_inc(wt_ps, 1)
            pe.wait_ge(wt_sb, 1)
            pe.wait_ge(loaded[4], 16)
            pe.wait_ge(loaded[11], 16)
            pe.wait_ge(w_ready, 5)

            def split_product(dst, w, cols, q):
                mm(dst, w[1][:, cols], xm_hi[q][:, :], start=True, stop=False)
                mm(dst, w[0][:, cols], xm_lo[q][:, :], start=False, stop=False)
                return mm(dst, w[0][:, cols], xm_hi[q][:, :], start=False, stop=True)

            def down(s, k):
                wait(pe, "hid_done", s, k + 1)
                if k == 0:
                    wait(pe, "y2t_sb", s - 1)
                mm(ps_y[:, :], w_down[:, k * D:k * D + D], hid[k % 2][:, :],
                   start=(k == 0), stop=(k == UNITS - 1)).then_inc(sems["down_ps"], 1)

            def step(s, q, att, moe, tail):
                p = 1 - q
                if tail:
                    wait(pe, "y2t_sb", s - 2)
                    wait(pe, "qs_done", s - 1)
                    for t in range(T):
                        i = nc.tensor.transpose(ps_t[:, tb(t)], y2_t[:, tb(t)], ident)
                    i.then_inc(sems["y2_ps"], 1)
                for k in range(UNITS):
                    if moe:
                        if k == 0:
                            wait(pe, "xmlo_done", s - 1)
                            wait(pe, "ct_sb", s - 1)
                        if k < PAIRS:
                            if k >= 1:
                                wait(pe, "cbc_done", s - 1, k)
                            else:
                                wait(pe, "cbc_done", s - 2)
                            mm(ps_c[:, :], sel[:, tb(k)], comb_t[p][:, :], start=True,
                               stop=True).then_inc(sems["c_ps"], 1)
                        if k >= 1:
                            wait(pe, "sil_done", s - 1, k)
                        else:
                            wait(pe, "sil_done", s - 2)
                        split_product(ps_g[:, :], w_gate, tb(k), p).then_inc(sems["gate_ps"], 1)
                        if k >= 1:
                            wait(pe, "hid_done", s - 1, k)
                        else:
                            wait(pe, "hid_done", s - 2)
                        split_product(ps_u[:, :], w_up, tb(k), p).then_inc(sems["up_ps"], 1)
                        if k >= 1:
                            down(s - 1, k - 1)
                    if att:
                        if k == 0:
                            wait(pe, "xn_done", s)
                            wait(pe, "lg_sb", s - 1)
                            for t in range(T):
                                i = nc.tensor.transpose(ps_a[:, tb(t)], xn[:, t, :], ident)
                            i.then_inc(sems["xnt_ps"], 1)
                        elif k in (1, 2):
                            b = k - 1
                            wait(pe, "xnt_sb", s)
                            if b:
                                wait(pe, "qkv_sb", s, b)
                            else:
                                wait(pe, "ct_sb", s - 1)
                            for r in range(R):
                                i = mm(ps_ab[:, 512 * r:512 * r + 3 * D], xn_t[:, tb(b * R + r)], wqkv[:, :],
                                       start=True, stop=True)
                            i.then_inc(sems["proj_ps"], 1)
                        elif k in (3, 4):
                            b = k - 3
                            wait(pe, "kv_done", s, b + 1)
                            if b:
                                wait(pe, "qs_done", s, b)
                            else:
                                wait(pe, "qs_done", s - 1)
                                if tail:
                                    wait(pe, "y2n_done", s - 2)
                            for c in range(KV // 512):
                                i = mm(ps_s[:, 512 * c:512 * c + 512], before,
                                       kv_w[:, 512 * c:512 * c + 512], start=True, stop=True)
                            i.then_inc(sems["pre_ps"], 1)
                        elif k == 6:
                            wait(pe, "retn_done", s)
                            wait(pe, "qkv_sb", s)
                            for t in range(T):
                                i = nc.tensor.transpose(ps_a[:, tb(t)], ret_n[:, tb(t)], ident)
                            i.then_inc(sems["rett_ps"], 1)
                            wait(pe, "rett_sb", s)
                            for t in range(T):
                                i = mm(ps_b[:, tb(t)], ret_t[:, tb(t)], wo[:, :], start=True, stop=True)
                            i.then_inc(sems["wo_ps"], 1)
                        elif k == 8:
                            wait(pe, "xm_done", s)
                            for t in range(T):
                                i = nc.tensor.transpose(ps_a[:, tb(t)], xm[:, t, :], ident)
                            i.then_inc(sems["xmt_ps"], 1)
                            wait(pe, "xmlo_done", s)
                            wait(pe, "yn_done", s)
                            split_product(ps_b, w_rout, slice(0, P), q).then_inc(sems["rout_ps"], 1)
                            wait(pe, "lgt_sb", s)
                            for t in range(T):
                                i = mm(ps_a[:, t * E:t * E + E], lg_t[:, tb(t)], ident[0:E, 0:E],
                                       start=True, stop=True)
                            i.then_inc(sems["lg_ps"], 1)
                            wait(pe, "clo_done", s)
                            for t in range(T):
                                i = nc.tensor.transpose(ps_b[0:2 * E, tb(t)],
                                                        comb_2[:, t, :].bitcast(fp32), ident)
                            i.then_inc(sems["ct_ps"], 1)
                if moe:
                    down(s - 1, UNITS - 1)

            steps(pe, step)


_INS = ['L0_attn_x', 'L0_attn_WQ', 'L0_attn_WK', 'L0_attn_WV', 'L0_attn_WO', 'L0_attn_gamma',
        'L0_attn_beta', 'L0_ffn_router_w', 'L0_ffn_router_bias', 'L0_ffn_up_proj', 'L0_ffn_gate_proj',
        'L0_ffn_down_proj', 'L0_ffn_sh_gate', 'L0_ffn_sh_up', 'L0_ffn_sh_down']


def kernel(**inputs):
    import concourse.bacc as _bacc
    from concourse.bass_utils import run_bass_kernel_spmd as _run

    nc = _bacc.Bacc("TRN2", target_bir_lowering=False, num_devices=1)
    arrays, args = {}, []
    for name in _INS:
        a = np.ascontiguousarray(inputs[name])
        arrays[f"in_{name}"] = a
        args.append(nc.dram_tensor(f"in_{name}", a.shape, mybir.dt.from_np(a.dtype), kind="ExternalInput").ap())
    table = constants()
    arrays["tables"] = table
    args.append(nc.dram_tensor("tables", table.shape, mybir.dt.float32, kind="ExternalInput").ap())
    args.append(nc.dram_tensor("out_0", (B, S, D), mybir.dt.float32, kind="ExternalOutput").ap())
    build(nc, *args)
    r = _run(nc, [arrays], core_ids=[0])
    return r.results[0]["out_0"]
```

```python
import numpy as np
import concourse.bass as bass
from concourse import mybir
from concourse.alu_op_type import AluOpType as ALU
from contextlib import ExitStack

B, S, D, H = 16, 256, 128, 16
DH = D // H
E, F = 16, 64
P = 128
NB = 2
G = B // NB
R = S // P
T = NB * R
N = T * P
UNITS = E * F // P + 1
PAIRS = UNITS - 1
EPS = 1e-5
KV = H * DH * DH


def constants():
    pos = np.arange(S, dtype=np.float32)
    expo = np.arange(0, DH, 2, dtype=np.float32) / np.float32(DH)
    angle = (np.float32(10.0) ** (np.float32(-4.0) * expo)).astype(np.float32)
    turn = (pos[:, None] * angle[None, :]).astype(np.float32).astype(np.float64)
    cos, sin = np.cos(turn), np.sin(turn)
    scale = (1.0 - 2.0 ** (-5.0 - np.arange(H))).astype(np.float64)
    grow = scale[None, :] ** (np.arange(S)[:, None] - S // 2)
    cq = np.zeros((S, 2, H, DH))
    sq = np.zeros((S, 2, H, DH))
    for n, w in enumerate((grow, 1.0 / grow)):
        cq[:, n, :, 0::2] = cos[:, None, :] * w[:, :, None]
        cq[:, n, :, 1::2] = cos[:, None, :] * w[:, :, None]
        sq[:, n, :, 0::2] = -sin[:, None, :] * w[:, :, None]
        sq[:, n, :, 1::2] = sin[:, None, :] * w[:, :, None]
    cq = cq.reshape(P, R * 2 * D)
    sq = sq.reshape(P, R * 2 * D)
    before = np.triu(np.ones((P, P)), 1)
    ident = np.eye(P)
    count = np.broadcast_to(np.arange(E), (P, E))
    sel = np.zeros((P, PAIRS, P))
    for r in range(2 * E):
        for m in range(P):
            if (r % E) // 2 < PAIRS and (r % E) % 2 == m // F:
                sel[r, (r % E) // 2, m] = 1.0
    parts = [cq, sq, before, ident, count, sel.reshape(P, PAIRS * P)]
    return np.concatenate(parts, axis=1).astype(np.float32)


CC = [0]
for _w in (R * 2 * D, R * 2 * D, P, P, E, PAIRS * P):
    CC.append(CC[-1] + _w)


def build(nc, x, WQ, WK, WV, WO, gamma, beta, router_w, router_bias, up_proj, gate_proj,
          down_proj, sh_gate, sh_up, sh_down, consts, out):
    fp32 = mybir.dt.float32
    f32r = mybir.dt.float32r
    u32 = mybir.dt.uint32
    i32 = mybir.dt.int32
    ACT = mybir.ActivationFunctionType
    AX = mybir.AxisListType.X

    with ExitStack() as ctx:
        def sb(name, shape, dt=fp32):
            return ctx.enter_context(nc.sbuf_tensor(name, shape, dt))

        def pb(name, width=512):
            return ctx.enter_context(nc.psum_tensor(name, [P, width], fp32))

        def sem(name):
            return ctx.enter_context(nc.semaphore(name))

        cst = sb("cst", [P, CC[5]])
        sel_in = sb("sel_in", [2 * E, PAIRS * P])
        rot_c = cst[:, CC[0]:CC[1]].rearrange("p (r n) -> p r n", r=R)
        rot_s = cst[:, CC[1]:CC[2]].rearrange("p (r n) -> p r n", r=R)
        before = cst[:, CC[2]:CC[3]]
        ident = cst[:, CC[3]:CC[4]]
        count = cst[:, CC[4]:CC[5]]
        sel = sb("sel", [2 * E, PAIRS * P], f32r)
        w_in = sb("w_in", [P, 7, P])
        g_in = sb("g_in", [P, E * F])
        u_in = sb("u_in", [P, E * F])
        wqkv = sb("wqkv", [P, 3 * D])
        wo = sb("wo", [P, D])
        w_gate = [sb(f"w_gate{i}", [P, UNITS * P], f32r) for i in range(2)]
        w_up = [sb(f"w_up{i}", [P, UNITS * P], f32r) for i in range(2)]
        w_rout = [sb(f"w_rout{i}", [P, P], f32r) for i in range(2)]
        w_down = sb("w_down", [P, UNITS * D])
        gam = sb("gam", [P, 1])
        bet = sb("bet", [P, 1])
        rbias = sb("rbias", [E, 1])
        neghalf = sb("neghalf", [P, T * H])
        eps_t = sb("eps_t", [P, T * H])
        minus1 = sb("minus1", [P, T])

        x_ln = sb("x_ln", [P, T, D])
        x_res = sb("x_res", [P, T, D])
        ln1_s = sb("ln1_s", [P, T, 6])
        ln1_m = sb("ln1_m", [P, T, 2])
        ln1_r = sb("ln1_r", [P, T])
        ln1_b = sb("ln1_b", [P, T])
        xn = sb("xn", [P, T, D])
        xn_t = sb("xn_t", [P, N])
        qkv = sb("qkv", [P, NB, R, 3 * D])
        ra = sb("ra", [P, R, 2 * D])
        rb = sb("rb", [P, R, 2 * D])
        qk = sb("qk", [P, NB, R, 2 * D])
        kv_a = sb("kv_a", [P, KV])
        kv_b = sb("kv_b", [P, KV])
        kv_w = sb("kv_w", [P, KV])
        qs = sb("qs", [P, R, KV])
        ret = sb("ret", [P, NB, R, D])
        dp = sb("dp", [P, NB, R + 1, D])
        dots = sb("dots", [P, NB, (R + 1) * H])
        near = sb("near", [P, NB, R, D])
        near2 = sb("near2", [P, NB, D])
        ret_f = sb("ret_f", [P, T * D])
        gn_mu = sb("gn_mu", [P, T * H])
        ret_c = sb("ret_c", [P, T * D])
        gn_sq = sb("gn_sq", [P, T * D])
        gn_v = sb("gn_v", [P, T * H])
        gn_r = sb("gn_r", [P, T * H])
        gn_i = sb("gn_i", [P, T * H], i32)
        gn_h = sb("gn_h", [P, T * H])
        gn_t = sb("gn_t", [P, T * H])
        ret_n = sb("ret_n", [P, T * D])
        ret_t = sb("ret_t", [P, N])
        y_s = sb("y_s", [P, T, 6])
        y_m = sb("y_m", [P, T, 2])
        y_r = sb("y_r", [P, T])
        y_b = sb("y_b", [P, T])
        y_n = sb("y_n", [P, T, D])
        x1 = [sb(f"x1_{i}", [P, T, D]) for i in range(2)]
        ln2_s = sb("ln2_s", [P, T, 6])
        ln2_m = sb("ln2_m", [P, T, 2])
        ln2_r = sb("ln2_r", [P, T])
        ln2_b = sb("ln2_b", [P, T])
        xm = sb("xm", [P, T, D])
        xm_hi = [sb(f"xm_hi{i}", [P, N], f32r) for i in range(2)]
        xm_lo = [sb(f"xm_lo{i}", [P, N], f32r) for i in range(2)]

        lg_t = sb("lg_t", [E, N])
        lg = sb("lg", [P, T, E])
        top = sb("top", [P, T, 8])
        idx = sb("idx", [P, T, 8], u32)
        idx_f = sb("idx_f", [P, T, 2])
        gap = sb("gap", [P, T])
        th = sb("th", [P, T])
        prob = sb("prob", [P, T, 2])
        hot = sb("hot", [P, T, 2, E])
        hot_p = sb("hot_p", [P, T, 2, E])
        comb = sb("comb", [P, T, E])
        comb_2 = sb("comb_2", [P, T, 2 * E], f32r)
        comb_t = [sb(f"comb_t{i}", [2 * E, N], f32r) for i in range(2)]

        sil = [sb(f"sil{i}", [P, N]) for i in range(2)]
        cbc = [sb(f"cbc{i}", [P, N]) for i in range(2)]
        silc = [sb(f"silc{i}", [P, N]) for i in range(2)]
        hid = [sb(f"hid{i}", [P, N]) for i in range(2)]
        y2_t = sb("y2_t", [P, N])
        y2_s = sb("y2_s", [P, T, 6])
        y2_m = sb("y2_m", [P, T, 2])
        y2_r = sb("y2_r", [P, T])
        y2_b = sb("y2_b", [P, T])
        y2_n = sb("y2_n", [P, T, D])
        x2 = sb("x2", [P, T, D])
        carrier = sb("carrier", [P, 1])

        ps_g = pb("ps_g")
        ps_u = pb("ps_u")
        ps_c = pb("ps_c")
        ps_y = pb("ps_y")
        ps_s = pb("ps_s", 1024)
        ps_ab = pb("ps_ab", 1024)
        ps_a, ps_b = ps_ab[:, 0:512], ps_ab[:, 512:1024]
        ps_s0, ps_s1 = ps_s[:, 0:512], ps_s[:, 512:1024]

        RSQ = 11
        PER = dict(
            x_in=16, xres_in=16, ln1_st=1, ln1_mv=1, ln1_rs=3, xn_done=1, xnt_ps=1, xnt_sb=1,
            proj_ps=NB, qkv_sb=NB, rot_ab=NB, qk_done=NB, kv_ab=NB, kv_done=NB, pre_ps=NB, qs_done=NB,
            ret_done=NB, dp_done=NB, dots_done=NB, near_ab=NB, near_done=NB,
            retf_done=1, mu_done=1, retc_done=1, sq_done=1, gnv_done=1, gnr_done=RSQ, retn_done=1,
            rett_ps=1, rett_sb=1, wo_ps=1, y_st=1, y_mv=1, y_rs=3, yn_done=1, x1_done=1,
            ln2_st=1, ln2_mv=1, ln2_rs=3, xm_done=1, xmt_ps=1, xmhi_done=1, xmlo_done=1,
            rout_ps=1, lgt_sb=1, lg_ps=1, lg_sb=1, top_done=1, idx_done=1, gap_done=1, th_done=1,
            prob_done=1, idxf_done=1, hot_done=1, hotp_done=1, comb_done=1, chi_done=1, clo_done=1,
            ct_ps=1, ct_sb=1,
            gate_ps=UNITS, up_ps=UNITS, c_ps=PAIRS, sil_done=UNITS, cbc_done=PAIRS, silc_done=PAIRS,
            hid_done=UNITS, down_ps=UNITS, y2t_sb=1, y2_ps=1, y2_st=1, y2_mv=1, y2_rs=3,
            y2n_done=1, x2_done=1, stored=16)
        sems = {k: sem(k) for k in PER}
        loaded = {k: sem(f"ld_{k}") for k in (
            "cst", "sel", "wq", "wk", "wv", "wo", "gate", "up", "shg", "shu", "shd", "rout", "down",
            "gam", "bet", "rbias")}
        wt_ps = sem("wt_ps")
        wt_sb = sem("wt_sb")
        w_high = sem("w_high")
        w_low = sem("w_low")
        small_ready = sem("small_ready")

        def wait(eng, name, g, n=None):
            n = PER[name] if n is None else n
            if not isinstance(g, int) or g >= 0:
                eng.wait_ge(sems[name], g * PER[name] + n)

        def wait_before(eng, name, g, n, back=1):
            while n <= back:
                g, n = g - 1, n + PER[name]
            wait(eng, name, g, n - back)

        x_v = x.rearrange("n (p r) d -> p n (r d)", r=R)
        out_v = out.rearrange("n (p r) d -> p n (r d)", r=R)

        def batches(view, g):
            if isinstance(g, int):
                return view[:, NB * g:NB * g + NB, :]
            return view[:, bass.ds(g * NB, NB), :]

        def tb(t):
            return slice(t * P, t * P + P)

        def pairs(ap):
            return ap.rearrange("p (n c) -> p n c", c=2)

        DEPTH = 3

        def run(eng, plan, depth=DEPTH):
            plan = sorted(plan, key=lambda item: item[0] % UNITS)

            def step(s, q):
                for slot, op in plan:
                    off = int(slot // UNITS)
                    g = s - off
                    if not isinstance(s, int) or 0 <= g < G:
                        op(g, (q - off) % 2)

            for s in range(DEPTH + 1):
                step(s, s % 2)
            with eng.Fori((DEPTH + 1) // 2, G // 2) as i:
                step(i * 2, 0)
                step(i * 2 + 1, 1)
            for s in range(G, G + depth):
                step(s, s % 2)

        XN, PROJ, PRE, RET, WO_, XM, ROUT, LG, CT = 1.5, (2.3, 3.3), (7.3, 10.3), 14.9, 15.9, 18.8, 19.9, 20.5, 21.6
        MOE = 22
        Y2 = MOE + UNITS + 1.6
        BANKS = {
            "a": [(XN, "xnt_sb", 1), (PROJ[0], "qkv_sb", 1), (PROJ[1], "qkv_sb", 2), (XM, "xmlo_done", 1),
                  (LG, "lg_sb", 1)],
            "b": [(PROJ[0], "qkv_sb", 1), (PROJ[1], "qkv_sb", 2), (WO_, "yn_done", 1), (ROUT, "lgt_sb", 1),
                  (CT, "ct_sb", 1)],
            "s0": [(PRE[0], "qs_done", 1), (PRE[1], "qs_done", 2), (RET, "rett_sb", 1)],
            "s1": [(PRE[0], "qs_done", 1), (PRE[1], "qs_done", 2), (Y2, "y2n_done", 1)],
        }

        def bank_read(eng, bank, slot, g):
            found = []
            for other, name, n in BANKS[bank]:
                first = int(-((slot - other) // UNITS)) if other != slot else 1
                found += [(other - UNITS * back, back, name, n) for back in range(first, first + 4)]
            for _, back, name, n in sorted(found, reverse=True):
                if not isinstance(g, int) or 0 <= g - back < G:
                    return wait(eng, name, g - back, n)

        block = ctx.enter_context(nc.Block())

        @block.sync
        def _(sp):
            def load(name, dst, src):
                sp.dma_start(dst, src).then_inc(loaded[name], 16)

            def load_x(s, q):
                wait(sp, "xn_done", s - 1)
                sp.dma_start(x_ln[:, :, :].rearrange("p (n r) d -> p n (r d)", r=R),
                             batches(x_v, s)).then_inc(sems["x_in"], 16)

            def load_res(s, q):
                wait(sp, "x1_done", s - 1)
                sp.dma_start(x_res[:, :, :].rearrange("p (n r) d -> p n (r d)", r=R),
                             batches(x_v, s)).then_inc(sems["xres_in"], 16)

            def store(s, q):
                wait(sp, "x2_done", s)
                sp.dma_start(batches(out_v, s), x2[:, :, :].rearrange("p (n r) d -> p n (r d)", r=R)
                             ).then_inc(sems["stored"], 16)

            def weights(s, q):
                if not (isinstance(s, int) and s == 0):
                    return
                load("cst", cst[:, :], consts[:, 0:CC[5]])
                for i, (n, w) in enumerate((("wq", WQ), ("wk", WK), ("wv", WV))):
                    load(n, w_in[:, i, :], w.rearrange("h u d -> (h u) d"))
                load("wo", wo[:, :], WO)
                load("shg", w_in[:, 3, :], sh_gate)
                load("shu", w_in[:, 4, :], sh_up)
                load("shd", w_in[:, 5, :], sh_down)
                sp.wait_ge(small_ready, 1)
                load("rout", w_in[0:E, 6, :], router_w)
                load("gate", g_in[:, :].rearrange("p (e f) -> p e f", f=F), gate_proj.rearrange("e d f -> d e f"))
                load("up", u_in[:, :].rearrange("p (e f) -> p e f", f=F), up_proj.rearrange("e d f -> d e f"))
                load("sel", sel_in[:, :], consts[0:2 * E, CC[5]:CC[6]])
                load("down", w_down[:, 0:PAIRS * D].rearrange("p (e d) -> p e d", d=D),
                     down_proj.rearrange("(n e) f d -> (e f) n d", e=2))

            run(sp, [(0.0, load_x), (0.1, weights), (UNITS + 0.2, load_res), (4 * UNITS + 0.3, store)],
                DEPTH + 1)
            sp.wait_ge(sems["stored"], 16 * G)

        @block.gpsimd
        def _(pool):
            nc.gpsimd.memset(w_in[:, 6, :], 0.0).then_inc(small_ready, 1)
            nc.gpsimd.memset(eps_t[:, :], EPS)
            nc.gpsimd.memset(minus1[:, :], -1.0)
            nc.gpsimd.memset(neghalf[:, :], -0.5).then_inc(small_ready, 1)
            for n, dst, src in (("gam", gam, gamma), ("bet", bet, beta), ("rbias", rbias, router_bias)):
                pool.dma_start(dst[:, :], src.rearrange("(p a) -> p a", a=1)).then_inc(loaded[n], 16)
            pool.wait_ge(small_ready, 2)

            def rstd_bias(g, name, mv_name, mv, r, bias):
                wait(pool, mv_name, g)
                nc.gpsimd.tensor_tensor(bias[:, :], mv[:, :, 0], minus1[:, :], ALU.mult)
                nc.gpsimd.tensor_tensor(r[:, :], mv[:, :, 1], eps_t[:, 0:T], ALU.add).then_inc(sems[name], 1)
                wait(pool, name, g, 1)
                nc.gpsimd.tensor_tensor(r[:, :], r[:, :], neghalf[:, 0:T], ALU.pow).then_inc(sems[name], 1)
                wait(pool, name, g, 2)
                nc.gpsimd.tensor_tensor(bias[:, :], bias[:, :], r[:, :], ALU.mult).then_inc(sems[name], 1)

            def outer(b, r, dst):
                k = qk[:, b, r, D:2 * D].rearrange("p (h u) -> p h u", u=DH)
                v = qkv[:, b, r, 2 * D:3 * D].rearrange("p (h v) -> p h v", v=DH)
                return nc.gpsimd.tensor_tensor(
                    dst[:, :].rearrange("p (h u v) -> p h u v", u=DH, v=DH),
                    k.unsqueeze(3).broadcast_to([P, H, DH, DH]),
                    v.unsqueeze(2).broadcast_to([P, H, DH, DH]), ALU.mult)

            def outer_a(b):
                def op(g, q):
                    wait(pool, "qk_done", g, b + 1)
                    wait_before(pool, "kv_done", g, b + 1)
                    outer(b, 0, kv_a)
                return op

            def outer_b(b):
                def op(g, q):
                    wait(pool, "qk_done", g, b + 1)
                    outer(b, 1, kv_b).then_inc(sems["kv_ab"], 1)
                return op

            def outer_sum(b):
                def op(g, q):
                    wait(pool, "kv_ab", g, b + 1)
                    wait_before(pool, "pre_ps", g, b + 1)
                    nc.gpsimd.tensor_tensor(kv_w[:, :], kv_a[:, :], kv_b[:, :],
                                            ALU.add).then_inc(sems["kv_done"], 1)
                return op

            def near_terms(b):
                def op(g, q):
                    wait(pool, "dots_done", g, b + 1)
                    wait(pool, "retf_done", g - 1)
                    d = dots[:, b, :].rearrange("p (n h) -> p n h", h=H)
                    v = qkv[:, b, :, 2 * D:3 * D].rearrange("p r (h v) -> p r h v", v=DH)
                    for r in range(R):
                        nc.gpsimd.tensor_tensor(near[:, b, r, :].rearrange("p (h v) -> p h v", v=DH),
                                                d[:, r, :].unsqueeze(2).broadcast_to([P, H, DH]),
                                                v[:, 0, :, :], ALU.mult)
                    nc.gpsimd.tensor_tensor(near2[:, b, :].rearrange("p (h v) -> p h v", v=DH),
                                            d[:, R, :].unsqueeze(2).broadcast_to([P, H, DH]),
                                            v[:, 1, :, :], ALU.mult).then_inc(sems["near_ab"], 1)
                    wait(pool, "near_ab", g, b + 1)
                    nc.gpsimd.tensor_tensor(near[:, b, 1, :], near[:, b, 1, :], near2[:, b, :],
                                            ALU.add).then_inc(sems["near_done"], 1)
                return op

            def first_residual(g, q):
                wait(pool, "yn_done", g)
                wait(pool, "xres_in", g)
                wait(pool, "x2_done", g - 2)
                wait(pool, "xm_done", g - 2)
                nc.gpsimd.tensor_tensor(x1[q][:, :, :], y_n[:, :, :], x_res[:, :, :],
                                        ALU.add).then_inc(sems["x1_done"], 1)

            def second_residual(g, q):
                wait(pool, "y2n_done", g)
                wait(pool, "stored", g - 1)
                nc.gpsimd.tensor_tensor(x2[:, :, :], y2_n[:, :, :], x1[q][:, :, :],
                                        ALU.add).then_inc(sems["x2_done"], 1)

            def weigh(k):
                def op(g, q):
                    wait(pool, "sil_done", g, k + 1)
                    wait(pool, "cbc_done", g, k + 1)
                    if k < 2:
                        wait(pool, "hid_done", g - 1, PAIRS - 1 + k)
                    else:
                        wait(pool, "hid_done", g, k - 1)
                    nc.gpsimd.tensor_tensor(silc[k % 2][:, :], sil[(k + q) % 2][:, :], cbc[k % 2][:, :],
                                            ALU.mult).then_inc(sems["silc_done"], 1)
                return op

            run(pool, [
                (0.5, lambda g, q: rstd_bias(g, "ln1_rs", "ln1_mv", ln1_m, ln1_r, ln1_b)),
                (4.0, outer_a(0)), (4.6, outer_b(0)), (5.5, outer_sum(0)),
                (6.4, outer_a(1)), (7.5, outer_b(1)), (9.2, outer_sum(1)),
                (10.4, near_terms(0)), (11.4, near_terms(1)),
                (16.5, lambda g, q: rstd_bias(g, "y_rs", "y_mv", y_m, y_r, y_b)),
                (17.1, first_residual),
                (17.9, lambda g, q: rstd_bias(g, "ln2_rs", "ln2_mv", ln2_m, ln2_r, ln2_b)),
                *[(MOE + k + 0.8, weigh(k)) for k in range(PAIRS)],
                (Y2 + 0.7, lambda g, q: rstd_bias(g, "y2_rs", "y2_mv", y2_m, y2_r, y2_b)),
                (Y2 + 1.8, second_residual),
            ])

        @block.scalar
        def _(act):
            Copy, Identity = ACT.Copy, ACT.Identity
            activate = nc.scalar.activation

            def early_weights(g, q):
                if isinstance(g, int) and g == 0:
                    act.wait_ge(wt_ps, 1)
                    activate(wqkv[:, :], ps_g[:, 0:3 * D], Copy).then_inc(wt_sb, 1)

            def late_weights(g, q):
                if not (isinstance(g, int) and g == 0):
                    return
                act.wait_ge(wt_ps, 2)
                activate(w_gate[0][:, PAIRS * P:], ps_u[:, 0:P], Copy)
                activate(w_up[0][:, PAIRS * P:], ps_u[:, P:2 * P], Copy)
                activate(w_down[:, PAIRS * D:], ps_u[:, 2 * P:3 * P], Copy)
                activate(w_rout[0][:, :], ps_u[:, 3 * P:4 * P], Copy).then_inc(w_high, 1)
                act.wait_ge(loaded["gate"], 16)
                activate(w_gate[0][:, 0:PAIRS * P], g_in[:, :], Copy).then_inc(w_high, 1)
                act.wait_ge(loaded["up"], 16)
                activate(w_up[0][:, 0:PAIRS * P], u_in[:, :], Copy).then_inc(w_high, 1)
                act.wait_ge(loaded["sel"], 16)
                activate(sel[:, :], sel_in[:, :], Copy).then_inc(w_high, 1)
                for n in ("gam", "bet", "rbias"):
                    act.wait_ge(loaded[n], 16)

            def norm_rows(dst, src, r, b, done):
                for t in range(T):
                    i = activate(dst[:, t, :], src(t), Identity, bias=b[:, t:t + 1], scale=r[:, t:t + 1])
                i.then_inc(sems[done], 1)

            def norm_x(g, q):
                wait(act, "ln1_rs", g)
                wait(act, "xnt_ps", g - 1)
                norm_rows(xn, lambda t: x_ln[:, t, :], ln1_r, ln1_b, "xn_done")

            def take_xn(g, q):
                wait(act, "xnt_ps", g)
                wait(act, "proj_ps", g - 1)
                activate(xn_t[:, :], ps_a, Copy).then_inc(sems["xnt_sb"], 1)

            def take_qkv(b):
                def op(g, q):
                    wait(act, "proj_ps", g, b + 1)
                    wait(act, "near_done", g - 1, b + 1)
                    wait(act, "kv_ab", g - 1, b + 1)
                    wait(act, "qk_done", g - 1, b + 1)
                    activate(qkv[:, b, :, :],
                             ps_ab[:, :].rearrange("p (r n) -> p r n", r=R)[:, :, 0:3 * D],
                             Copy).then_inc(sems["qkv_sb"], 1)
                return op

            def square(g, q):
                wait(act, "retc_done", g)
                wait(act, "gnv_done", g - 1)
                activate(gn_sq[:, :], ret_c[:, :], ACT.Square, scale=DH ** -0.5).then_inc(sems["sq_done"], 1)

            def take_ret(g, q):
                wait(act, "rett_ps", g)
                wait(act, "wo_ps", g - 1)
                activate(ret_t[:, :], ps_s0, Identity, bias=bet[:, :], scale=gam[:, :]
                         ).then_inc(sems["rett_sb"], 1)

            def norm_y(g, q):
                wait(act, "y_rs", g)
                wait(act, "x1_done", g - 1)
                norm_rows(y_n, lambda t: ps_b[:, tb(t)], y_r, y_b, "yn_done")

            def norm_x1(g, q):
                wait(act, "ln2_rs", g)
                wait(act, "xmt_ps", g - 1)
                norm_rows(xm, lambda t: x1[q][:, t, :], ln2_r, ln2_b, "xm_done")

            def take_xm(g, q):
                wait(act, "xmt_ps", g)
                wait(act, "up_ps", g - 2)
                activate(xm_hi[q][:, :], ps_a, Copy).then_inc(sems["xmhi_done"], 1)

            def take_logits(g, q):
                wait(act, "rout_ps", g)
                wait(act, "lg_ps", g - 1)
                activate(lg_t[:, :], ps_b[0:E, :], Identity, bias=rbias[:, :]).then_inc(sems["lgt_sb"], 1)

            def tanh(g, q):
                wait(act, "gap_done", g)
                wait(act, "prob_done", g - 1)
                activate(th[:, :], gap[:, :], ACT.Tanh, scale=0.5).then_inc(sems["th_done"], 1)

            def take_comb(g, q):
                wait(act, "ct_ps", g)
                wait(act, "c_ps", g - 2)
                activate(comb_t[q][:, :], ps_b[0:2 * E, :], Copy).then_inc(sems["ct_sb"], 1)

            def take_c(k):
                def op(g, q):
                    wait(act, "c_ps", g, k + 1)
                    wait_before(act, "silc_done", g, k + 1, 2)
                    activate(cbc[k % 2][:, :], ps_c[:, :], Copy).then_inc(sems["cbc_done"], 1)
                return op

            def silu(k):
                def op(g, q):
                    wait(act, "gate_ps", g, k + 1)
                    if k == 0:
                        wait(act, "silc_done", g - 1)
                    elif k == 1:
                        wait(act, "hid_done", g - 1)
                    else:
                        wait(act, "silc_done", g, k - 1)
                    activate(sil[(k + q) % 2][:, :], ps_g[:, :], ACT.Silu).then_inc(sems["sil_done"], 1)
                return op

            def take_y2(g, q):
                wait(act, "down_ps", g)
                wait(act, "y2_ps", g - 1)
                activate(y2_t[:, :], ps_y[:, :], Copy).then_inc(sems["y2t_sb"], 1)

            def norm_y2(g, q):
                wait(act, "y2_rs", g)
                wait(act, "x2_done", g - 1)
                norm_rows(y2_n, lambda t: ps_s1[:, tb(t)], y2_r, y2_b, "y2n_done")

            run(act, [
                (0.0, early_weights), (1.0, norm_x), (1.9, take_xn),
                (2.6, take_qkv(0)), (3.5, take_qkv(1)), (4.0, late_weights),
                (12.9, square), (15.2, take_ret), (16.9, norm_y), (18.5, norm_x1),
                (19.2, take_xm), (20.2, take_logits), (21.0, tanh), (21.9, take_comb),
                *[(MOE + k + 0.3, take_c(k)) for k in range(PAIRS)],
                *[(MOE + k + 0.5, silu(k)) for k in range(UNITS)],
                (MOE + UNITS + 1.1, take_y2), (Y2 + 1.0, norm_y2),
            ])

        @block.vector
        def _(dve):
            tt = nc.vector.tensor_tensor

            def late_weights(g, q):
                if not (isinstance(g, int) and g == 0):
                    return
                dve.wait_ge(w_high, 1)
                for n, w in enumerate((w_gate, w_up)):
                    tt(w[1][:, PAIRS * P:], ps_u[:, tb(n)], w[0][:, PAIRS * P:].bitcast(fp32), ALU.subtract)
                tt(w_rout[1][:, :], ps_u[:, 3 * P:4 * P], w_rout[0][:, :].bitcast(fp32),
                   ALU.subtract).then_inc(w_low, 1)
                dve.wait_ge(w_high, 2)
                tt(w_gate[1][:, 0:PAIRS * P], g_in[:, :], w_gate[0][:, 0:PAIRS * P].bitcast(fp32), ALU.subtract)
                dve.wait_ge(w_high, 3)
                tt(w_up[1][:, 0:PAIRS * P], u_in[:, :], w_up[0][:, 0:PAIRS * P].bitcast(fp32),
                   ALU.subtract).then_inc(w_low, 1)

            def carry_wait():
                nc.vector.memset(carrier[:, :], 0.0)

            def stats(g, st, mv, sem_st, sem_mv, src):
                for t in range(T):
                    i = nc.vector.bn_stats(st[:, t, :], src(t))
                i.then_inc(sems[sem_st], 1)
                wait(dve, sem_st, g)
                carry_wait()
                for t in range(T):
                    i = nc.vector.bn_aggr(mv[:, t, :], st[:, t, :])
                i.then_inc(sems[sem_mv], 1)

            def stats_x(g, q):
                wait(dve, "x_in", g)
                wait(dve, "ln1_rs", g - 1)
                stats(g, ln1_s, ln1_m, "ln1_st", "ln1_mv", lambda t: x_ln[:, t, :])

            def rotate(b):
                def op(g, q):
                    wait(dve, "qkv_sb", g, b + 1)
                    wait_before(dve, "qk_done", g, b + 1)
                    for r in range(R):
                        tt(pairs(rb[:, r, :]), pairs(qkv[:, b, r, 0:2 * D])[:, :, ::-1], pairs(rot_s[:, r, :]),
                           ALU.mult)
                    tt(ra[:, :, :], qkv[:, b, :, 0:2 * D], rot_c, ALU.mult).then_inc(sems["rot_ab"], 1)
                    wait(dve, "rot_ab", g, b + 1)
                    wait(dve, "kv_ab", g - 1, b + 1)
                    wait(dve, "qs_done", g - 1, b + 1)
                    tt(qk[:, b, :, :], ra[:, :, :], rb[:, :, :], ALU.add).then_inc(sems["qk_done"], 1)
                return op

            def near_dots(b):
                def op(g, q):
                    wait(dve, "dots_done", g - 1, b + 1)
                    wait(dve, "qk_done", g, b + 1)
                    tt(dp[:, b, 0:R, :], qk[:, b, :, 0:D],
                       qk[:, b, 0, D:2 * D].unsqueeze(1).broadcast_to([P, R, D]), ALU.mult)
                    tt(dp[:, b, R, :], qk[:, b, 1, 0:D], qk[:, b, 1, D:2 * D], ALU.mult
                       ).then_inc(sems["dp_done"], 1)
                    wait(dve, "dp_done", g, b + 1)
                    wait(dve, "near_ab", g - 1, b + 1)
                    nc.vector.tensor_reduce(dots[:, b, :],
                                            dp[:, b, :, :].rearrange("p n (h u) -> p (n h) u", u=DH),
                                            AX, ALU.add).then_inc(sems["dots_done"], 1)
                return op

            def apply_q(b):
                def op(g, q):
                    wait_before(dve, "ret_done", g, b + 1)
                    wait(dve, "pre_ps", g, b + 1)
                    for r in range(R):
                        i = tt(qs[:, r, :].rearrange("p (n v) -> p n v", v=DH),
                               ps_s[:, :].rearrange("p (n v) -> p n v", v=DH),
                               qk[:, b, r, 0:D].unsqueeze(2).broadcast_to([P, D, DH]), ALU.mult)
                    i.then_inc(sems["qs_done"], 1)
                return op

            def sum_q(b):
                def op(g, q):
                    wait(dve, "qs_done", g, b + 1)
                    wait(dve, "retf_done", g - 1)
                    for r in range(R):
                        i = nc.vector.tensor_reduce(ret[:, b, r, :].rearrange("p (h v) -> p h v", v=DH),
                                                    qs[:, r, :].rearrange("p (h u v) -> p h v u", u=DH, v=DH),
                                                    AX, ALU.add)
                    i.then_inc(sems["ret_done"], 1)
                return op

            heads = lambda a: a[:, :].rearrange("p (n v) -> p n v", v=DH)
            wide = lambda a: a[:, :].unsqueeze(2).broadcast_to([P, T * H, DH])

            def add_near(g, q):
                wait(dve, "near_done", g)
                wait(dve, "ret_done", g)
                wait(dve, "retc_done", g - 1)
                tt(ret_f[:, :], ret[:, :, :, :].rearrange("p n r d -> p (n r d)"),
                   near[:, :, :, :].rearrange("p n r d -> p (n r d)"), ALU.add).then_inc(sems["retf_done"], 1)

            def head_mean(g, q):
                wait(dve, "retf_done", g)
                nc.vector.tensor_reduce(gn_mu[:, :], heads(ret_f), AX, ALU.add).then_inc(sems["mu_done"], 1)

            def centre(g, q):
                wait(dve, "mu_done", g)
                wait(dve, "retn_done", g - 1)
                nc.vector.scalar_tensor_tensor(heads(ret_c), wide(gn_mu), -1.0 / DH, heads(ret_f),
                                               ALU.mult, ALU.add).then_inc(sems["retc_done"], 1)

            def head_var(g, q):
                wait(dve, "sq_done", g)
                nc.vector.tensor_reduce(gn_v[:, :], heads(gn_sq), AX, ALU.add).then_inc(sems["gnv_done"], 1)

            def head_rstd(n):
                def op(g, q):
                    if n == 0:
                        wait(dve, "gnv_done", g)
                        i = nc.vector.tensor_scalar(gn_t[:, :], gn_v[:, :], EPS, None, ALU.add)
                        i.then_inc(sems["gnr_done"], 1)
                        return
                    wait(dve, "gnr_done", g, n)
                    if n == 1:
                        nc.vector.tensor_scalar(gn_h[:, :], gn_t[:, :], -0.5, None, ALU.mult)
                        i = nc.vector.tensor_scalar(gn_r[:, :].bitcast(i32), gn_t[:, :].bitcast(i32),
                                                    -0.5, float(0x5F3759DF), ALU.mult, ALU.add)
                    elif n % 3 == 2:
                        i = tt(gn_t[:, :], gn_r[:, :], gn_r[:, :], ALU.mult)
                    elif n % 3 == 0:
                        i = tt(gn_t[:, :], gn_t[:, :], gn_h[:, :], ALU.mult)
                    else:
                        i = nc.vector.scalar_tensor_tensor(gn_r[:, :], gn_t[:, :], 1.5, gn_r[:, :],
                                                           ALU.add, ALU.mult)
                    i.then_inc(sems["gnr_done"], 1)
                return op

            def scale_heads(g, q):
                wait(dve, "gnr_done", g)
                wait(dve, "rett_ps", g - 1)
                tt(heads(ret_n), heads(ret_c), wide(gn_r), ALU.mult).then_inc(sems["retn_done"], 1)

            def stats_y(g, q):
                wait(dve, "wo_ps", g)
                stats(g, y_s, y_m, "y_st", "y_mv", lambda t: ps_b[:, tb(t)])

            def stats_x1(g, q):
                wait(dve, "x1_done", g)
                stats(g, ln2_s, ln2_m, "ln2_st", "ln2_mv", lambda t: x1[q][:, t, :])

            def xm_low(g, q):
                wait(dve, "xmhi_done", g)
                wait(dve, "up_ps", g - 2)
                tt(xm_lo[q][:, :], ps_a, xm_hi[q][:, :].bitcast(fp32), ALU.subtract
                   ).then_inc(sems["xmlo_done"], 1)

            def top_two(g, q):
                wait(dve, "lg_ps", g)
                nc.vector.tensor_copy(lg[:, :, :].rearrange("p t e -> p (t e)"),
                                      ps_a[:, 0:T * E]).then_inc(sems["lg_sb"], 1)
                wait(dve, "lg_sb", g)
                carry_wait()
                for t in range(T):
                    i = nc.vector.max(top[:, t, :], lg[:, t, :])
                i.then_inc(sems["top_done"], 1)
                wait(dve, "top_done", g)
                tt(gap[:, :], top[:, :, 1], top[:, :, 0], ALU.subtract).then_inc(sems["gap_done"], 1)
                for t in range(T):
                    i = nc.vector.max_index(idx[:, t, :], top[:, t, :], lg[:, t, :])
                i.then_inc(sems["idx_done"], 1)
                wait(dve, "idx_done", g)
                nc.vector.tensor_copy(idx_f[:, :, :], idx[:, :, 0:2]).then_inc(sems["idxf_done"], 1)

            def combine(g, q):
                wait(dve, "idxf_done", g)
                flat = lambda a: a[:, :, :, :].rearrange("p t c e -> p (t c) e")
                over_e = lambda a: a[:, :, :].rearrange("p t c -> p (t c)").unsqueeze(2).broadcast_to([P, 2 * T, E])
                tt(flat(hot), count.unsqueeze(1).broadcast_to([P, 2 * T, E]), over_e(idx_f),
                   ALU.is_equal).then_inc(sems["hot_done"], 1)
                wait(dve, "th_done", g)
                nc.vector.tensor_scalar(prob[:, :, 0], th[:, :], -0.5, 0.5, ALU.mult, ALU.add)
                nc.vector.tensor_scalar(prob[:, :, 1], th[:, :], 0.5, 0.5, ALU.mult,
                                        ALU.add).then_inc(sems["prob_done"], 1)
                wait(dve, "prob_done", g)
                tt(flat(hot_p), flat(hot), over_e(prob), ALU.mult).then_inc(sems["hotp_done"], 1)
                wait(dve, "hotp_done", g)
                tt(comb[:, :, :], hot_p[:, :, 0, :], hot_p[:, :, 1, :], ALU.add).then_inc(sems["comb_done"], 1)
                wait(dve, "comb_done", g)
                wait(dve, "ct_ps", g - 1)
                nc.vector.tensor_copy(comb_2[:, :, 0:E], comb[:, :, :]).then_inc(sems["chi_done"], 1)
                wait(dve, "chi_done", g)
                tt(comb_2[:, :, E:2 * E], comb[:, :, :], comb_2[:, :, 0:E].bitcast(fp32),
                   ALU.subtract).then_inc(sems["clo_done"], 1)

            def hidden(k):
                def op(g, q):
                    wait(dve, "up_ps", g, k + 1)
                    if k < PAIRS:
                        wait(dve, "silc_done", g, k + 1)
                    else:
                        wait(dve, "sil_done", g, k + 1)
                    wait_before(dve, "down_ps", g, k + 1, 2)
                    other = silc[k % 2] if k < PAIRS else sil[(k + q) % 2]
                    tt(hid[(k + q) % 2][:, :], ps_u[:, :], other[:, :], ALU.mult).then_inc(sems["hid_done"], 1)
                return op

            def stats_y2(g, q):
                wait(dve, "y2_ps", g)
                stats(g, y2_s, y2_m, "y2_st", "y2_mv", lambda t: ps_s1[:, tb(t)])

            run(dve, [
                (0.3, stats_x), (3.2, rotate(0)), (4.2, rotate(1)), (4.9, late_weights),
                (5.2, near_dots(0)), (5.3, near_dots(1)),
                (8.2, apply_q(0)), (9.2, sum_q(0)), (10.7, apply_q(1)), (11.3, sum_q(1)),
                (12.2, add_near), (12.3, head_mean), (12.4, centre), (13.3, head_var),
                *[(13.4 + 0.1 * n, head_rstd(n)) for n in range(RSQ)], (14.6, scale_heads),
                (16.3, stats_y), (17.5, stats_x1), (19.4, xm_low), (20.8, top_two), (21.2, combine),
                *[(MOE + k + 1.1, hidden(k)) for k in range(UNITS)],
                (Y2 + 0.5, stats_y2),
            ])

        @block.tensor
        def _(pe):
            mm = nc.tensor.matmul

            def transposes(dst, src):
                for t in range(T):
                    i = nc.tensor.transpose(dst[:, tb(t)], src(t), ident)
                return i

            def early_weights(g, q):
                if not (isinstance(g, int) and g == 0):
                    return
                pe.wait_ge(loaded["cst"], 16)
                for i, n in enumerate(("wq", "wk", "wv")):
                    pe.wait_ge(loaded[n], 16)
                    t_ = nc.tensor.transpose(ps_g[:, tb(i)], w_in[:, i, :], ident)
                t_.then_inc(wt_ps, 1)

            def late_weights(g, q):
                if not (isinstance(g, int) and g == 0):
                    return
                for i, n in enumerate(("shg", "shu", "shd", "rout")):
                    pe.wait_ge(loaded[n], 16)
                    t_ = nc.tensor.transpose(ps_u[:, tb(i)], w_in[:, 3 + i, :], ident)
                t_.then_inc(wt_ps, 1)

            def split_product(dst, w, cols, q):
                mm(dst, w[1][:, cols], xm_hi[q][:, :], start=True, stop=False)
                mm(dst, w[0][:, cols], xm_lo[q][:, :], start=False, stop=False)
                return mm(dst, w[0][:, cols], xm_hi[q][:, :], start=False, stop=True)

            def turn_xn(g, q):
                wait(pe, "xn_done", g)
                bank_read(pe, "a", XN, g)
                transposes(ps_a, lambda t: xn[:, t, :]).then_inc(sems["xnt_ps"], 1)

            def project(b):
                def op(g, q):
                    if isinstance(g, int) and g == 0 and b == 0:
                        pe.wait_ge(wt_sb, 1)
                    wait(pe, "xnt_sb", g)
                    bank_read(pe, "a", PROJ[b], g)
                    bank_read(pe, "b", PROJ[b], g)
                    for r in range(R):
                        i = mm(ps_ab[:, 512 * r:512 * r + 3 * D], xn_t[:, tb(b * R + r)], wqkv[:, :],
                               start=True, stop=True)
                    i.then_inc(sems["proj_ps"], 1)
                return op

            def prefix(b):
                def op(g, q):
                    wait(pe, "kv_done", g, b + 1)
                    bank_read(pe, "s0", PRE[b], g)
                    bank_read(pe, "s1", PRE[b], g)
                    for c in range(KV // 512):
                        i = mm(ps_s[:, 512 * c:512 * c + 512], before, kv_w[:, 512 * c:512 * c + 512],
                               start=True, stop=True)
                    i.then_inc(sems["pre_ps"], 1)
                return op

            def turn_ret(g, q):
                wait(pe, "retn_done", g)
                bank_read(pe, "s0", RET, g)
                transposes(ps_s0, lambda t: ret_n[:, tb(t)]).then_inc(sems["rett_ps"], 1)

            def project_out(g, q):
                if isinstance(g, int) and g == 0:
                    pe.wait_ge(loaded["wo"], 16)
                wait(pe, "rett_sb", g)
                bank_read(pe, "b", WO_, g)
                for t in range(T):
                    i = mm(ps_b[:, tb(t)], ret_t[:, tb(t)], wo[:, :], start=True, stop=True)
                i.then_inc(sems["wo_ps"], 1)

            def turn_xm(g, q):
                wait(pe, "xm_done", g)
                bank_read(pe, "a", XM, g)
                transposes(ps_a, lambda t: xm[:, t, :]).then_inc(sems["xmt_ps"], 1)

            def route(g, q):
                if isinstance(g, int) and g == 0:
                    pe.wait_ge(w_high, 4)
                    pe.wait_ge(w_low, 2)
                    pe.wait_ge(loaded["down"], 16)
                wait(pe, "xmlo_done", g)
                bank_read(pe, "b", ROUT, g)
                split_product(ps_b, w_rout, slice(0, P), q).then_inc(sems["rout_ps"], 1)

            def turn_logits(g, q):
                wait(pe, "lgt_sb", g)
                bank_read(pe, "a", LG, g)
                for t in range(T):
                    i = mm(ps_a[:, t * E:t * E + E], lg_t[:, tb(t)], ident[0:E, 0:E], start=True, stop=True)
                i.then_inc(sems["lg_ps"], 1)

            def turn_comb(g, q):
                wait(pe, "clo_done", g)
                bank_read(pe, "b", CT, g)
                for t in range(T):
                    i = nc.tensor.transpose(ps_b[0:2 * E, tb(t)], comb_2[:, t, :].bitcast(fp32), ident)
                i.then_inc(sems["ct_ps"], 1)

            def spread(k):
                def op(g, q):
                    if k == 0:
                        wait(pe, "ct_sb", g)
                    wait_before(pe, "cbc_done", g, k + 1)
                    mm(ps_c[:, :], sel[:, tb(k)], comb_t[q][:, :], start=True,
                       stop=True).then_inc(sems["c_ps"], 1)
                return op

            def gate(k):
                def op(g, q):
                    wait_before(pe, "sil_done", g, k + 1)
                    split_product(ps_g[:, :], w_gate, tb(k), q).then_inc(sems["gate_ps"], 1)
                return op

            def up(k):
                def op(g, q):
                    wait_before(pe, "hid_done", g, k + 1)
                    split_product(ps_u[:, :], w_up, tb(k), q).then_inc(sems["up_ps"], 1)
                return op

            def down(k):
                def op(g, q):
                    wait(pe, "hid_done", g, k + 1)
                    if k == 0:
                        wait(pe, "y2t_sb", g - 1)
                    mm(ps_y[:, :], w_down[:, k * D:k * D + D], hid[(k + q) % 2][:, :],
                       start=(k == 0), stop=(k == UNITS - 1)).then_inc(sems["down_ps"], 1)
                return op

            def turn_y2(g, q):
                wait(pe, "y2t_sb", g)
                bank_read(pe, "s1", Y2, g)
                transposes(ps_s1, lambda t: y2_t[:, tb(t)]).then_inc(sems["y2_ps"], 1)

            run(pe, [
                (0.0, early_weights), (XN, turn_xn), (PROJ[0], project(0)), (PROJ[1], project(1)),
                (3.5, late_weights), (PRE[0], prefix(0)), (PRE[1], prefix(1)),
                (RET, turn_ret), (WO_, project_out), (XM, turn_xm), (ROUT, route), (LG, turn_logits),
                (CT, turn_comb),
                *[(MOE + k + 0.05, spread(k)) for k in range(PAIRS)],
                *[(MOE + k + 0.15, gate(k)) for k in range(UNITS)],
                *[(MOE + k + 0.75, up(k)) for k in range(UNITS)],
                *[(MOE + k + 1.65, down(k)) for k in range(UNITS)],
                (Y2, turn_y2),
            ])


_INS = ['L0_attn_x', 'L0_attn_WQ', 'L0_attn_WK', 'L0_attn_WV', 'L0_attn_WO', 'L0_attn_gamma',
        'L0_attn_beta', 'L0_ffn_router_w', 'L0_ffn_router_bias', 'L0_ffn_up_proj', 'L0_ffn_gate_proj',
        'L0_ffn_down_proj', 'L0_ffn_sh_gate', 'L0_ffn_sh_up', 'L0_ffn_sh_down']


def kernel(**inputs):
    import concourse.bacc as _bacc
    from concourse.bass_utils import run_bass_kernel_spmd as _run

    nc = _bacc.Bacc("TRN2", target_bir_lowering=False, num_devices=1)
    arrays, args = {}, []
    for name in _INS:
        a = np.ascontiguousarray(inputs[name])
        arrays[f"in_{name}"] = a
        args.append(nc.dram_tensor(f"in_{name}", a.shape, mybir.dt.from_np(a.dtype), kind="ExternalInput").ap())
    table = constants()
    arrays["tables"] = table
    args.append(nc.dram_tensor("tables", table.shape, mybir.dt.float32, kind="ExternalInput").ap())
    args.append(nc.dram_tensor("out_0", (B, S, D), mybir.dt.float32, kind="ExternalOutput").ap())
    build(nc, *args)
    r = _run(nc, [arrays], core_ids=[0])
    return r.results[0]["out_0"]
```

```python
import numpy as np
import concourse.bass as bass
from concourse import mybir
from concourse.alu_op_type import AluOpType as ALU
from contextlib import ExitStack

B, S, D, H = 16, 256, 128, 16
DH = D // H
E, F = 16, 64
P = 128
NB = 2
G = B // NB
R = S // P
T = NB * R
N = T * P
UNITS = E * F // P + 1
PAIRS = UNITS - 1
EPS = 1e-5
KV = H * DH * DH


def constants():
    pos = np.arange(S, dtype=np.float32)
    expo = np.arange(0, DH, 2, dtype=np.float32) / np.float32(DH)
    angle = (np.float32(10.0) ** (np.float32(-4.0) * expo)).astype(np.float32)
    turn = (pos[:, None] * angle[None, :]).astype(np.float32).astype(np.float64)
    cos, sin = np.cos(turn), np.sin(turn)
    scale = (1.0 - 2.0 ** (-5.0 - np.arange(H))).astype(np.float64)
    grow = scale[None, :] ** (np.arange(S)[:, None] - S // 2)
    cq = np.zeros((S, 2, H, DH))
    sq = np.zeros((S, 2, H, DH))
    for n, w in enumerate((grow, 1.0 / grow)):
        cq[:, n, :, 0::2] = cos[:, None, :] * w[:, :, None]
        cq[:, n, :, 1::2] = cos[:, None, :] * w[:, :, None]
        sq[:, n, :, 0::2] = -sin[:, None, :] * w[:, :, None]
        sq[:, n, :, 1::2] = sin[:, None, :] * w[:, :, None]
    cq = cq.reshape(P, R * 2 * D)
    sq = sq.reshape(P, R * 2 * D)
    before = np.triu(np.ones((P, P)), 1)
    ident = np.eye(P)
    count = np.broadcast_to(np.arange(E), (P, E))
    sel = np.zeros((P, PAIRS, P))
    for r in range(2 * E):
        for m in range(P):
            if (r % E) // 2 < PAIRS and (r % E) % 2 == m // F:
                sel[r, (r % E) // 2, m] = 1.0
    parts = [cq, sq, before, ident, count, sel.reshape(P, PAIRS * P)]
    return np.concatenate(parts, axis=1).astype(np.float32)


CC = [0]
for _w in (R * 2 * D, R * 2 * D, P, P, E, PAIRS * P):
    CC.append(CC[-1] + _w)


AT = dict(
    turn_wqkv=1.58, turn_shared=9.06, turn_xn=1.96, project=(6.62, 10.1), prefix=(14.71, 17),
    turn_ret=23.07, project_out=23.65, turn_xm=26.51, route=27.04, turn_comb=28.33, spread=29.03,
    gate=28.95, up=30.28, down=31.53,
    gate_low=24.28, up_low=30.56, ln1_rstd=2.45, outer_a=(11.34, 14.19), outer_b=(13.02, 16.41),
    near_terms=19.8, y_rstd=26.47, first_residual=26.86, ln2_rstd=27.63, combine=29.72, weigh=32.1,
    y2_rstd=44.05, second_residual=44.72,
    take_wqk=5.9, shared_high=23.35, gate_high=12.27, up_high=26.29, take_sel=24.69, mean_x=2.22,
    var_x=2.27, norm_x=3.89, take_xn=7.6, take_qkv=(9.77, 12.79), square=23.41, take_ret=25.1,
    var_y=26.02, norm_y=26.37, norm_x1=28.82, take_xm=29.1, tanh=30.47, take_comb=31.56, take_c=31.94,
    silu=31.59, take_y2=42.33, var_y2=43.08, norm_y2=44.3,
    centre_wv=1.21, centre_wo=5.67, shared_low=21.72, centre_down=21.55, rotate=(7.07, 9.52),
    near_dots=12.56, outer_sum=(12.48, 12.63), apply_q=(13.54, 16.78), sum_q=(14.88, 17.34),
    add_near=18.14, head_var=19.64, head_rstd=(19.65, 0.12), scale_heads=21.09, stats_x1=23.77,
    xm_low=25.46, top_two=25.93, hidden=29.11,
)


def build(nc, x, WQ, WK, WV, WO, gamma, beta, router_w, router_bias, up_proj, gate_proj,
          down_proj, sh_gate, sh_up, sh_down, consts, out):
    fp32 = mybir.dt.float32
    f32r = mybir.dt.float32r
    u32 = mybir.dt.uint32
    i32 = mybir.dt.int32
    ACT = mybir.ActivationFunctionType
    AX = mybir.AxisListType.X

    with ExitStack() as ctx:
        def sb(name, shape, dt=fp32):
            return ctx.enter_context(nc.sbuf_tensor(name, shape, dt))

        def pb(name, width=512):
            return ctx.enter_context(nc.psum_tensor(name, [P, width], fp32))

        def sem(name):
            return ctx.enter_context(nc.semaphore(name))

        cst = sb("cst", [P, CC[5]])
        sel_in = sb("sel_in", [2 * E, PAIRS * P])
        rot_c = cst[:, CC[0]:CC[1]].rearrange("p (r n) -> p r n", r=R)
        rot_s = cst[:, CC[1]:CC[2]].rearrange("p (r n) -> p r n", r=R)
        before = cst[:, CC[2]:CC[3]]
        ident = cst[:, CC[3]:CC[4]]
        count = cst[:, CC[4]:CC[5]]
        sel = sb("sel", [2 * E, PAIRS * P], f32r)
        w_in = sb("w_in", [P, 7, P])
        g_in = sb("g_in", [P, E * F])
        u_in = sb("u_in", [P, E * F])
        wqkv = sb("wqkv", [P, 3 * D])
        wo = sb("wo", [P, D])
        w_gate = [sb(f"w_gate{i}", [P, UNITS * P], f32r) for i in range(2)]
        w_up = [sb(f"w_up{i}", [P, UNITS * P], f32r) for i in range(2)]
        w_rout = [sb(f"w_rout{i}", [P, P], f32r) for i in range(2)]
        w_down = sb("w_down", [P, UNITS * D])
        wv_sum = sb("wv_sum", [P, H])
        wo_sum = sb("wo_sum", [P, 1])
        down_sum = sb("down_sum", [P, UNITS])
        gam = sb("gam", [P, 1])
        bet = sb("bet", [P, 1])
        rbias = sb("rbias", [P, E])
        neghalf = sb("neghalf", [P, T * H])
        eps_t = sb("eps_t", [P, T * H])
        minus1 = sb("minus1", [P, T])
        root_d = sb("root_d", [P, T])

        x_ln = sb("x_ln", [P, T, D])
        x_res = sb("x_res", [P, T, D])
        x_sum = sb("x_sum", [P, T, D])
        x_sq = sb("x_sq", [P, T, D])
        ln1_m = sb("ln1_m", [P, T])
        ln1_v = sb("ln1_v", [P, T])
        ln1_r = sb("ln1_r", [P, T])
        ln1_b = sb("ln1_b", [P, T])
        xn = sb("xn", [P, T, D])
        xn_t = sb("xn_t", [P, N])
        qkv = [sb(f"qkv{i}", [P, NB, R, 3 * D]) for i in range(2)]
        ra = sb("ra", [P, R, 2 * D])
        rb = sb("rb", [P, R, 2 * D])
        qk = [sb(f"qk{i}", [P, NB, R, 2 * D]) for i in range(2)]
        kv_a = [sb(f"kv_a{b}", [P, KV]) for b in range(NB)]
        kv_b = [sb(f"kv_b{b}", [P, KV]) for b in range(NB)]
        kv_w = [sb(f"kv_w{b}", [P, KV]) for b in range(NB)]
        qs = sb("qs", [P, R, KV])
        ret = sb("ret", [P, NB, R, D])
        dp = sb("dp", [P, NB, R + 1, D])
        dots = sb("dots", [P, NB, (R + 1) * H])
        near = sb("near", [P, NB, R, D])
        near2 = sb("near2", [P, NB, D])
        ret_f = sb("ret_f", [P, T * D])
        gn_sq = sb("gn_sq", [P, T * D])
        gn_v = sb("gn_v", [P, T * H])
        gn_r = sb("gn_r", [P, T * H])
        gn_h = sb("gn_h", [P, T * H])
        gn_t = sb("gn_t", [P, T * H])
        ret_n = sb("ret_n", [P, T * D])
        ret_t = sb("ret_t", [P, N])
        y_v = sb("y_v", [P, T])
        y_r = sb("y_r", [P, T])
        y_n = sb("y_n", [P, T, D])
        x1 = [sb(f"x1_{i}", [P, T, D]) for i in range(2)]
        ln2_s = sb("ln2_s", [P, T, 6])
        ln2_m = sb("ln2_m", [P, T, 2])
        ln2_r = sb("ln2_r", [P, T])
        ln2_b = sb("ln2_b", [P, T])
        y_sq = sb("y_sq", [P, T, D])
        y2_sq = sb("y2_sq", [P, T, D])
        xm = sb("xm", [P, T, D])
        xm_hi = [sb(f"xm_hi{i}", [P, N], f32r) for i in range(2)]
        xm_lo = [sb(f"xm_lo{i}", [P, N], f32r) for i in range(2)]

        lg = sb("lg", [P, T, E])
        top = sb("top", [P, T, 8])
        idx = sb("idx", [P, T, 8], u32)
        idx_f = sb("idx_f", [P, T, 2])
        gap = sb("gap", [P, T])
        th = sb("th", [P, T])
        prob = sb("prob", [P, T, 2])
        hot = sb("hot", [P, T, 2, E])
        hot_p = sb("hot_p", [P, T, 2, E])
        comb = sb("comb", [P, T, E])
        comb_2 = sb("comb_2", [P, T, 2 * E], f32r)
        comb_t = [sb(f"comb_t{i}", [2 * E, N], f32r) for i in range(2)]

        sil = [sb(f"sil{i}", [P, N]) for i in range(2)]
        cbc = [sb(f"cbc{i}", [P, N]) for i in range(2)]
        silc = [sb(f"silc{i}", [P, N]) for i in range(2)]
        hid = [sb(f"hid{i}", [P, N]) for i in range(2)]
        y2 = sb("y2", [P, N])
        y2_v = sb("y2_v", [P, T])
        y2_r = sb("y2_r", [P, T])
        y2_n = sb("y2_n", [P, T, D])
        x2 = sb("x2", [P, T, D])
        carrier = sb("carrier", [P, 1])

        ps_g = pb("ps_g")
        ps_u = pb("ps_u")
        ps_c = pb("ps_c")
        ps_y = pb("ps_y")
        ps_s = pb("ps_s", 1024)
        ps_ab = pb("ps_ab", 1024)
        ps_a, ps_b = ps_ab[:, 0:512], ps_ab[:, 512:1024]
        ps_s0, ps_s1 = ps_s[:, 0:512], ps_s[:, 512:1024]

        RSQ = 11
        PER = dict(
            x_in=16, xres_in=16, ln1_st=1, ln1_mv=1, ln1_rs=3, xn_done=1, xnt_ps=1, xnt_sb=1,
            proj_ps=NB, qkv_sb=NB, rot_ab=NB, qk_done=NB, kv_ab=NB, kv_done=NB, pre_ps=NB, qs_done=NB,
            ret_done=NB, dp_done=1, dots_done=1, near_ab=1, near_done=1,
            retf_done=1, sq_done=1, gnv_done=1, gnr_done=RSQ, retn_done=1,
            rett_ps=1, rett_sb=1, wo_ps=1, y_var=1, y_rs=2, yn_done=1, x1_done=1,
            ln2_st=1, ln2_mv=1, ln2_rs=3, xm_done=1, xmt_ps=1, xmhi_done=1, xmlo_done=1,
            lg_ps=1, lg_sb=1, top_done=1, idx_done=1, gap_done=1, th_done=1,
            prob_done=1, idxf_done=1, hot_done=1, hotp_done=1, comb_done=1, clo_done=1,
            ct_ps=1, ct_sb=1,
            gate_ps=UNITS, up_ps=UNITS, c_ps=PAIRS, sil_done=UNITS, cbc_done=PAIRS, silc_done=PAIRS,
            hid_done=UNITS, down_ps=UNITS, y2_sb=1, y2_var=1, y2_rs=2,
            y2n_done=1, x2_done=1, stored=16)
        LOADS = ("ident", "cst", "sel", "wq", "wk", "wv", "wo", "gate", "up", "shg", "shu", "shd", "rout",
                 "down", "gam", "bet", "rbias")
        ONCE = dict(
            wqkv_ps=1, wqk_sb=1, wv_sum_done=1, wv_done=1, shared_ps=1, shared_hi=1, shared_lo=1, gate_hi=1,
            gate_lo=1, up_hi=1, up_lo=1, sel_done=1, wo_sum_done=1, wo_done=1, down_sum_done=1, down_done=1,
            rout_zero=1, small_ready=1, **{f"ld_{k}": 16 for k in LOADS})
        PER.update(ONCE)
        sems = {k: sem(k) for k in PER}

        AHEAD = dict(up_ps=1, c_ps=1, y2n_done=1, y2_rs=1, x2_done=1, stored=16)

        def upto(name, g, n=None):
            signals = g * PER[name] + (PER[name] if n is None else n)
            if isinstance(signals, int) and signals <= 0:
                return 0
            return signals + AHEAD.get(name, 0)

        def due(value):
            return not isinstance(value, int) or value > 0

        x_v = x.rearrange("n (p r) d -> p n (r d)", r=R)
        out_v = out.rearrange("n (p r) d -> p n (r d)", r=R)

        def batches(view, g):
            if isinstance(g, int):
                return view[:, NB * g:NB * g + NB, :]
            return view[:, bass.ds(g * NB, NB), :]

        def tb(t):
            return slice(t * P, t * P + P)

        def pairs(ap):
            return ap.rearrange("p (n c) -> p n c", c=2)

        DEPTH = 3

        def once(op):
            return lambda g, q: op() if isinstance(g, int) and g == 0 else None

        def run(eng, plan):
            plan = sorted(plan, key=lambda item: item[0] % UNITS)

            def peeled(steps):
                for s in steps:
                    for slot, op in plan:
                        g = s - int(slot // UNITS)
                        if 0 <= g < G:
                            op(g, g % 2)

            def step(s, q):
                for slot, op in plan:
                    off = int(slot // UNITS)
                    op(s - off, (q - off) % 2)

            peeled(range(0, DEPTH + 1))
            with eng.Fori((DEPTH + 1) // 2, G // 2) as i:
                step(i * 2, 0)
                step(i * 2 + 1, 1)
            peeled(range(G, 2 * G))

        BANKS = {
            "a": [(AT["turn_xn"], "xnt_sb", 1), (AT["project"][0], "qkv_sb", 1),
                  (AT["project"][1], "qkv_sb", 2), (AT["turn_xm"], "xmlo_done", 1),
                  (AT["route"], "lg_sb", 1)],
            "b": [(AT["project"][0], "qkv_sb", 1), (AT["project"][1], "qkv_sb", 2),
                  (AT["project_out"], "yn_done", 1), (AT["turn_comb"], "ct_sb", 1)],
            "s0": [(AT["prefix"][0], "qs_done", 1), (AT["prefix"][1], "qs_done", 2),
                   (AT["turn_ret"], "rett_sb", 1)],
            "s1": [(AT["prefix"][0], "qs_done", 1), (AT["prefix"][1], "qs_done", 2)],
        }

        def reader(bank, slot, g):
            uses = []
            for other, name, n in BANKS[bank]:
                latest = int((other - slot) // UNITS) + 1
                uses += [(other - UNITS * back, back, name, n) for back in range(latest, latest + 4)]
            for _, back, name, n in sorted(uses, reverse=True):
                if not isinstance(g, int) or 0 <= g - back < G:
                    return name, upto(name, g - back, n)
            return None

        block = ctx.enter_context(nc.Block())

        @block.sync
        def _(sp):
            def load(name, dst, src):
                sp.dma_start(dst, src).then_inc(sems[f"ld_{name}"], 16)

            def load_x(s, q):
                if due(c := upto("xn_done", s - 1)):
                    sp.wait_ge(sems["xn_done"], c)
                sp.dma_start(x_ln[:, :, :].rearrange("p (n r) d -> p n (r d)", r=R),
                             batches(x_v, s)).then_inc(sems["x_in"], 16)

            def load_res(s, q):
                if isinstance(s, int) and s == 0:
                    sp.wait_ge(sems["stored"], AHEAD["stored"])
                if due(c := upto("x1_done", s - 1)):
                    sp.wait_ge(sems["x1_done"], c)
                sp.dma_start(x_res[:, :, :].rearrange("p (n r) d -> p n (r d)", r=R),
                             batches(x_v, s)).then_inc(sems["xres_in"], 16)

            def store(s, q):
                if isinstance(s, int) and s == G - 1:
                    for b in range(NB):
                        sp.wait_ge(sems["x2_done"], upto("x2_done", s) + b)
                        sp.dma_start(out_v[:, NB * s + b:NB * s + b + 1, :],
                                     x2[:, b * R:b * R + R, :].rearrange("p (n r) d -> p n (r d)", r=R)
                                     ).then_inc(sems["stored"], 16)
                    return
                sp.wait_ge(sems["x2_done"], upto("x2_done", s))
                sp.dma_start(batches(out_v, s), x2[:, :, :].rearrange("p (n r) d -> p n (r d)", r=R)
                             ).then_inc(sems["stored"], 16)

            def first_weights():
                load("ident", ident, consts[:, CC[3]:CC[4]])
                for i, (n, w) in enumerate((("wq", WQ), ("wk", WK), ("wv", WV))):
                    load(n, w_in[:, i, :], w.rearrange("h u d -> (h u) d"))
                load("cst", cst[:, 0:CC[3]], consts[:, 0:CC[3]])

            def second_weights():
                load("shg", w_in[:, 3, :], sh_gate)
                load("shu", w_in[:, 4, :], sh_up)
                load("shd", w_in[:, 5, :], sh_down)
                sp.wait_ge(sems["rout_zero"], upto("rout_zero", 0))
                load("rout", w_in[0:E, 6, :], router_w)
                load("gate", g_in[:, :].rearrange("p (e f) -> p e f", f=F),
                     gate_proj.rearrange("e d f -> d e f"))
                load("up", u_in[:, :].rearrange("p (e f) -> p e f", f=F), up_proj.rearrange("e d f -> d e f"))
                load("wo", wo[:, :], WO)
                load("down", w_down[:, 0:PAIRS * D].rearrange("p (e d) -> p e d", d=D),
                     down_proj.rearrange("(n e) f d -> (e f) n d", e=2))
                for n, dst, src in (("gam", gam, gamma), ("bet", bet, beta)):
                    load(n, dst[:, :], src.rearrange("(p a) -> p a", a=1))
                load("rbias", rbias[:, :], router_bias.rearrange("(a e) -> a e", a=1).broadcast_to([P, E]))
                load("sel", sel_in[:, :], consts[0:2 * E, CC[5]:CC[6]])
                sp.dma_start(count, consts[:, CC[4]:CC[5]]).then_inc(sems["stored"], AHEAD["stored"])

            run(sp, [(0.0, load_x), (0.1, once(first_weights)), (0.2, once(second_weights)),
                     (UNITS + 0.2, load_res), (4 * UNITS + 0.3, store)])
            sp.wait_ge(sems["stored"], upto("stored", G - 1) + 16 * (NB - 1))

        @block.gpsimd
        def _(pool):
            tt = nc.gpsimd.tensor_tensor

            def small_tables():
                nc.gpsimd.memset(w_in[:, 6, :], 0.0).then_inc(sems["rout_zero"], 1)
                nc.gpsimd.memset(eps_t[:, :], EPS).then_inc(sems["y2_rs"], AHEAD["y2_rs"])
                nc.gpsimd.memset(minus1[:, :], -1.0).then_inc(sems["x2_done"], AHEAD["x2_done"])
                nc.gpsimd.memset(root_d[:, :], D ** 0.5)
                nc.gpsimd.memset(neghalf[:, :], -0.5).then_inc(sems["small_ready"], 1)
                pool.wait_ge(sems["small_ready"], upto("small_ready", 0))

            def gate_low():
                pool.wait_ge(sems["gate_hi"], upto("gate_hi", 0))
                nc.gpsimd.tensor_tensor(w_gate[1][:, 0:PAIRS * P], g_in[:, :],
                                        w_gate[0][:, 0:PAIRS * P].bitcast(fp32),
                                        ALU.subtract).then_inc(sems["gate_lo"], 1)

            def up_low():
                pool.wait_ge(sems["up_hi"], upto("up_hi", 0))
                nc.gpsimd.tensor_tensor(w_up[1][:, 0:PAIRS * P], u_in[:, :],
                                        w_up[0][:, 0:PAIRS * P].bitcast(fp32),
                                        ALU.subtract).then_inc(sems["up_lo"], 1)

            def rstd_bias(g, name, mv_name, mean, var, factor, r, bias):
                pool.wait_ge(sems[mv_name], upto(mv_name, g))
                nc.gpsimd.tensor_tensor(bias[:, :], mean, factor[:, :], ALU.mult)
                nc.gpsimd.tensor_tensor(r[:, :], var, eps_t[:, 0:T], ALU.add).then_inc(sems[name], 1)
                pool.wait_ge(sems[name], upto(name, g, 1))
                nc.gpsimd.tensor_tensor(r[:, :], r[:, :], neghalf[:, 0:T], ALU.pow).then_inc(sems[name], 1)
                pool.wait_ge(sems[name], upto(name, g, 2))
                nc.gpsimd.tensor_tensor(bias[:, :], bias[:, :], r[:, :], ALU.mult).then_inc(sems[name], 1)

            def rstd(g, name, var_name, var, r):
                pool.wait_ge(sems[var_name], upto(var_name, g))
                nc.gpsimd.tensor_tensor(r[:, :], var[:, :], eps_t[:, 0:T], ALU.add).then_inc(sems[name], 1)
                pool.wait_ge(sems[name], upto(name, g, 1))
                nc.gpsimd.tensor_tensor(r[:, :], r[:, :], neghalf[:, 0:T], ALU.pow).then_inc(sems[name], 1)

            def outer(q, b, r, dst):
                k = qk[q][:, b, r, D:2 * D].rearrange("p (h u) -> p h u", u=DH)
                v = qkv[q][:, b, r, 2 * D:3 * D].rearrange("p (h v) -> p h v", v=DH)
                return nc.gpsimd.tensor_tensor(
                    dst[:, :].rearrange("p (h u v) -> p h u v", u=DH, v=DH),
                    k.unsqueeze(3).broadcast_to([P, H, DH, DH]),
                    v.unsqueeze(2).broadcast_to([P, H, DH, DH]), ALU.mult)

            def outer_a(b):
                def op(g, q):
                    pool.wait_ge(sems["qk_done"], upto("qk_done", g, b + 1))
                    if due(c := upto("kv_done", g - 1, b + 1)):
                        pool.wait_ge(sems["kv_done"], c)
                    outer(q, b, 0, kv_a[b])
                return op

            def outer_b(b):
                def op(g, q):
                    pool.wait_ge(sems["qk_done"], upto("qk_done", g, b + 1))
                    outer(q, b, 1, kv_b[b]).then_inc(sems["kv_ab"], 1)
                return op

            def near_terms(g, q):
                pool.wait_ge(sems["dots_done"], upto("dots_done", g))
                if due(c := upto("retf_done", g - 1)):
                    pool.wait_ge(sems["retf_done"], c)
                d = dots[:, :, :].rearrange("p n (c h) -> p n c h", h=H)

                def term(dst, c, r):
                    return nc.gpsimd.tensor_tensor(
                        dst.rearrange("p n (h v) -> p n h v", v=DH),
                        d[:, :, c, :].unsqueeze(3).broadcast_to([P, NB, H, DH]),
                        qkv[q][:, :, r, 2 * D:3 * D].rearrange("p n (h v) -> p n h v", v=DH), ALU.mult)
                term(near[:, :, 0, :], 0, 0)
                term(near[:, :, 1, :], 1, 0)
                term(near2[:, :, :], R, 1).then_inc(sems["near_ab"], 1)
                pool.wait_ge(sems["near_ab"], upto("near_ab", g))
                nc.gpsimd.tensor_tensor(near[:, :, 1, :], near[:, :, 1, :], near2[:, :, :],
                                        ALU.add).then_inc(sems["near_done"], 1)

            def first_residual(g, q):
                pool.wait_ge(sems["yn_done"], upto("yn_done", g))
                pool.wait_ge(sems["xres_in"], upto("xres_in", g))
                if due(c := upto("x2_done", g - 2)):
                    pool.wait_ge(sems["x2_done"], c)
                if due(c := upto("xm_done", g - 2)):
                    pool.wait_ge(sems["xm_done"], c)
                nc.gpsimd.tensor_tensor(x1[q][:, :, :], y_n[:, :, :], x_res[:, :, :],
                                        ALU.add).then_inc(sems["x1_done"], 1)

            def second_residual(g, q):
                pool.wait_ge(sems["y2n_done"], upto("y2n_done", g))
                if due(c := upto("stored", g - 1)):
                    pool.wait_ge(sems["stored"], c)
                if isinstance(g, int) and g == G - 1:
                    for b in range(NB):
                        rows = slice(b * R, b * R + R)
                        tt(x2[:, rows, :], y2_n[:, rows, :], x1[q][:, rows, :],
                           ALU.add).then_inc(sems["x2_done"], 1)
                    return
                nc.gpsimd.tensor_tensor(x2[:, :, :], y2_n[:, :, :], x1[q][:, :, :],
                                        ALU.add).then_inc(sems["x2_done"], 1)

            def combine(g, q):
                flat = lambda a: a[:, :, :, :].rearrange("p t c e -> p (t c) e")
                p_over_e = prob[:, :, :].rearrange("p t c -> p (t c)").unsqueeze(2).broadcast_to([P, 2 * T, E])
                pool.wait_ge(sems["hot_done"], upto("hot_done", g))
                pool.wait_ge(sems["prob_done"], upto("prob_done", g))
                tt(flat(hot_p), flat(hot), p_over_e, ALU.mult).then_inc(sems["hotp_done"], 1)
                pool.wait_ge(sems["hotp_done"], upto("hotp_done", g))
                if due(c := upto("ct_ps", g - 1)):
                    pool.wait_ge(sems["ct_ps"], c)
                tt(comb[:, :, :], hot_p[:, :, 0, :], hot_p[:, :, 1, :], ALU.add)
                tt(comb_2[:, :, 0:E], hot_p[:, :, 0, :], hot_p[:, :, 1, :],
                   ALU.add).then_inc(sems["comb_done"], 1)
                pool.wait_ge(sems["comb_done"], upto("comb_done", g))
                tt(comb_2[:, :, E:2 * E], comb[:, :, :], comb_2[:, :, 0:E].bitcast(fp32),
                   ALU.subtract).then_inc(sems["clo_done"], 1)

            def weigh(k):
                def op(g, q):
                    pool.wait_ge(sems["sil_done"], upto("sil_done", g, k + 1))
                    pool.wait_ge(sems["cbc_done"], upto("cbc_done", g, k + 1))
                    if k < 2:
                        if due(c := upto("hid_done", g - 1, PAIRS - 1 + k)):
                            pool.wait_ge(sems["hid_done"], c)
                    else:
                        pool.wait_ge(sems["hid_done"], upto("hid_done", g, k - 1))
                    nc.gpsimd.tensor_tensor(silc[k % 2][:, :], sil[(k + q) % 2][:, :], cbc[k % 2][:, :],
                                            ALU.mult).then_inc(sems["silc_done"], 1)
                return op

            run(pool, [
                (0.0, once(small_tables)), (AT["gate_low"], once(gate_low)), (AT["up_low"], once(up_low)),
                (AT["ln1_rstd"], lambda g, q: rstd_bias(g, "ln1_rs", "ln1_mv", ln1_m[:, :], ln1_v[:, :],
                                                         root_d, ln1_r, ln1_b)),
                *[(AT["outer_a"][b], outer_a(b)) for b in range(NB)],
                *[(AT["outer_b"][b], outer_b(b)) for b in range(NB)],
                (AT["near_terms"], near_terms),
                (AT["y_rstd"], lambda g, q: rstd(g, "y_rs", "y_var", y_v, y_r)),
                (AT["first_residual"], first_residual),
                (AT["ln2_rstd"], lambda g, q: rstd_bias(g, "ln2_rs", "ln2_mv", ln2_m[:, :, 0], ln2_m[:, :, 1],
                                                         minus1, ln2_r, ln2_b)),
                (AT["combine"], combine), *[(AT["weigh"] + k, weigh(k)) for k in range(PAIRS)],
                (AT["y2_rstd"], lambda g, q: rstd(g, "y2_rs", "y2_var", y2_v, y2_r)),
                (AT["second_residual"], second_residual),
            ])

        @block.scalar
        def _(act):
            Copy, Identity = ACT.Copy, ACT.Identity
            activate = nc.scalar.activation

            def take_wqk():
                act.wait_ge(sems["wqkv_ps"], upto("wqkv_ps", 0))
                activate(wqkv[:, 0:2 * D], ps_g[:, 0:2 * D], Copy).then_inc(sems["wqk_sb"], 1)

            def shared_high():
                act.wait_ge(sems["shared_ps"], upto("shared_ps", 0))
                activate(w_gate[0][:, PAIRS * P:], ps_u[:, 0:P], Copy).then_inc(sems["y2n_done"], AHEAD["y2n_done"])
                activate(w_up[0][:, PAIRS * P:], ps_u[:, P:2 * P], Copy)
                activate(w_down[:, PAIRS * D:], ps_u[:, 2 * P:3 * P], Copy)
                activate(w_rout[0][:, :], ps_u[:, 3 * P:4 * P], Copy).then_inc(sems["shared_hi"], 1)

            def gate_high():
                act.wait_ge(sems["ld_gate"], upto("ld_gate", 0))
                activate(w_gate[0][:, 0:PAIRS * P], g_in[:, :], Copy).then_inc(sems["gate_hi"], 1)

            def up_high():
                act.wait_ge(sems["ld_up"], upto("ld_up", 0))
                activate(w_up[0][:, 0:PAIRS * P], u_in[:, :], Copy).then_inc(sems["up_hi"], 1)

            def take_sel():
                act.wait_ge(sems["ld_sel"], upto("ld_sel", 0))
                activate(sel[:, :], sel_in[:, :], Copy).then_inc(sems["sel_done"], 1)

            def norm_rows(dst, src, r, b, done):
                for t in range(T):
                    i = activate(dst[:, t, :], src(t), Identity, bias=b[:, t:t + 1], scale=r[:, t:t + 1])
                i.then_inc(sems[done], 1)

            def mean_x(g, q):
                act.wait_ge(sems["x_in"], upto("x_in", g))
                if due(c := upto("ln1_rs", g - 1)):
                    act.wait_ge(sems["ln1_rs"], c)
                for t in range(T):
                    i = activate(x_sum[:, t, :], x_ln[:, t, :], Copy, scale=-D ** -1.5,
                                 accum_out=ln1_m[:, t:t + 1])
                i.then_inc(sems["ln1_st"], 1)

            def var_x(g, q):
                act.wait_ge(sems["ln1_st"], upto("ln1_st", g))
                for t in range(T):
                    i = activate(x_sq[:, t, :], x_ln[:, t, :], ACT.Square, bias=ln1_m[:, t:t + 1],
                                 scale=D ** -0.5, accum_out=ln1_v[:, t:t + 1])
                i.then_inc(sems["ln1_mv"], 1)

            def norm_x(g, q):
                act.wait_ge(sems["ln1_rs"], upto("ln1_rs", g))
                if due(c := upto("xnt_ps", g - 1)):
                    act.wait_ge(sems["xnt_ps"], c)
                norm_rows(xn, lambda t: x_ln[:, t, :], ln1_r, ln1_b, "xn_done")

            def take_xn(g, q):
                act.wait_ge(sems["xnt_ps"], upto("xnt_ps", g))
                if due(c := upto("proj_ps", g - 1)):
                    act.wait_ge(sems["proj_ps"], c)
                activate(xn_t[:, :], ps_a, Copy).then_inc(sems["xnt_sb"], 1)

            def take_qkv(b):
                def op(g, q):
                    act.wait_ge(sems["proj_ps"], upto("proj_ps", g, b + 1))
                    if due(c := upto("near_done", g - 2)):
                        act.wait_ge(sems["near_done"], c)
                    if due(c := upto("kv_ab", g - 2, b + 1)):
                        act.wait_ge(sems["kv_ab"], c)
                    if due(c := upto("qk_done", g - 2, b + 1)):
                        act.wait_ge(sems["qk_done"], c)
                    activate(qkv[q][:, b, :, :],
                             ps_ab[:, :].rearrange("p (r n) -> p r n", r=R)[:, :, 0:3 * D],
                             Copy).then_inc(sems["qkv_sb"], 1)
                return op

            def square(g, q):
                act.wait_ge(sems["retf_done"], upto("retf_done", g))
                if due(c := upto("gnv_done", g - 1)):
                    act.wait_ge(sems["gnv_done"], c)
                activate(gn_sq[:, :], ret_f[:, :], ACT.Square, scale=DH ** -0.5).then_inc(sems["sq_done"], 1)

            def take_ret(g, q):
                if isinstance(g, int) and g == 0:
                    act.wait_ge(sems["ld_gam"], upto("ld_gam", 0))
                    act.wait_ge(sems["ld_bet"], upto("ld_bet", 0))
                act.wait_ge(sems["rett_ps"], upto("rett_ps", g))
                if due(c := upto("wo_ps", g - 1)):
                    act.wait_ge(sems["wo_ps"], c)
                activate(ret_t[:, :], ps_s0, Identity, bias=bet[:, :], scale=gam[:, :]
                         ).then_inc(sems["rett_sb"], 1)

            def variances(dst, squares, src, done):
                for t in range(T):
                    i = activate(squares[:, t, :], src(t), ACT.Square, scale=D ** -0.5,
                                 accum_out=dst[:, t:t + 1])
                i.then_inc(sems[done], 1)

            def scale_rows(dst, src, r, done):
                for t in range(T):
                    i = activate(dst[:, t, :], src(t), Copy, scale=r[:, t:t + 1])
                i.then_inc(sems[done], 1)

            def var_y(g, q):
                act.wait_ge(sems["wo_ps"], upto("wo_ps", g))
                if due(c := upto("y_rs", g - 1)):
                    act.wait_ge(sems["y_rs"], c)
                variances(y_v, y_sq, lambda t: ps_b[:, tb(t)], "y_var")

            def var_y2(g, q):
                act.wait_ge(sems["y2_sb"], upto("y2_sb", g))
                if due(c := upto("y2_rs", g - 1)):
                    act.wait_ge(sems["y2_rs"], c)
                variances(y2_v, y2_sq, lambda t: y2[:, tb(t)], "y2_var")

            def norm_y(g, q):
                act.wait_ge(sems["y_rs"], upto("y_rs", g))
                if due(c := upto("x1_done", g - 1)):
                    act.wait_ge(sems["x1_done"], c)
                scale_rows(y_n, lambda t: ps_b[:, tb(t)], y_r, "yn_done")

            def norm_x1(g, q):
                act.wait_ge(sems["ln2_rs"], upto("ln2_rs", g))
                if due(c := upto("xmt_ps", g - 1)):
                    act.wait_ge(sems["xmt_ps"], c)
                norm_rows(xm, lambda t: x1[q][:, t, :], ln2_r, ln2_b, "xm_done")

            def take_xm(g, q):
                act.wait_ge(sems["xmt_ps"], upto("xmt_ps", g))
                if due(c := upto("up_ps", g - 2)):
                    act.wait_ge(sems["up_ps"], c)
                activate(xm_hi[q][:, :], ps_a, Copy).then_inc(sems["xmhi_done"], 1)

            def tanh(g, q):
                act.wait_ge(sems["gap_done"], upto("gap_done", g))
                activate(th[:, :], gap[:, :], ACT.Tanh, scale=0.5).then_inc(sems["th_done"], 1)
                act.wait_ge(sems["th_done"], upto("th_done", g))
                if due(c := upto("hotp_done", g - 1)):
                    act.wait_ge(sems["hotp_done"], c)
                activate(prob[:, :, 0], th[:, :], Copy, bias=0.5, scale=-0.5)
                activate(prob[:, :, 1], th[:, :], Copy, bias=0.5, scale=0.5).then_inc(sems["prob_done"], 1)

            def take_comb(g, q):
                act.wait_ge(sems["ct_ps"], upto("ct_ps", g))
                if due(c := upto("c_ps", g - 2)):
                    act.wait_ge(sems["c_ps"], c)
                activate(comb_t[q][:, :], ps_b[0:2 * E, :], Copy).then_inc(sems["ct_sb"], 1)

            def take_c(k):
                def op(g, q):
                    act.wait_ge(sems["c_ps"], upto("c_ps", g, k + 1))
                    if due(c := upto("silc_done", g, k - 1)):
                        act.wait_ge(sems["silc_done"], c)
                    activate(cbc[k % 2][:, :], ps_c[:, :], Copy).then_inc(sems["cbc_done"], 1)
                return op

            def silu(k):
                def op(g, q):
                    act.wait_ge(sems["gate_ps"], upto("gate_ps", g, k + 1))
                    if k == 0:
                        if due(c := upto("silc_done", g - 1)):
                            act.wait_ge(sems["silc_done"], c)
                    elif k == 1:
                        if due(c := upto("hid_done", g - 1)):
                            act.wait_ge(sems["hid_done"], c)
                    else:
                        act.wait_ge(sems["silc_done"], upto("silc_done", g, k - 1))
                    activate(sil[(k + q) % 2][:, :], ps_g[:, :], ACT.Silu).then_inc(sems["sil_done"], 1)
                return op

            def take_y2(g, q):
                act.wait_ge(sems["down_ps"], upto("down_ps", g))
                if due(c := upto("y2n_done", g - 1)):
                    act.wait_ge(sems["y2n_done"], c)
                activate(y2[:, :], ps_y[:, :], Copy).then_inc(sems["y2_sb"], 1)

            def norm_y2(g, q):
                act.wait_ge(sems["y2_rs"], upto("y2_rs", g))
                if due(c := upto("x2_done", g - 1)):
                    act.wait_ge(sems["x2_done"], c)
                scale_rows(y2_n, lambda t: y2[:, tb(t)], y2_r, "y2n_done")

            run(act, [
                (AT["take_wqk"], once(take_wqk)), (AT["shared_high"], once(shared_high)),
                (AT["gate_high"], once(gate_high)), (AT["up_high"], once(up_high)),
                (AT["take_sel"], once(take_sel)), (AT["mean_x"], mean_x), (AT["var_x"], var_x),
                (AT["norm_x"], norm_x), (AT["take_xn"], take_xn),
                *[(AT["take_qkv"][b], take_qkv(b)) for b in range(NB)],
                (AT["square"], square), (AT["take_ret"], take_ret), (AT["var_y"], var_y),
                (AT["norm_y"], norm_y),
                (AT["norm_x1"], norm_x1), (AT["take_xm"], take_xm),
                (AT["tanh"], tanh), (AT["take_comb"], take_comb),
                *[(AT["take_c"] + k, take_c(k)) for k in range(PAIRS)],
                *[(AT["silu"] + k, silu(k)) for k in range(UNITS)],
                (AT["take_y2"], take_y2), (AT["var_y2"], var_y2), (AT["norm_y2"], norm_y2),
            ])

        @block.vector
        def _(dve):
            tt = nc.vector.tensor_tensor

            def centre(name, dst, src, sums, width):
                nc.vector.tensor_reduce(sums, src, AX, ALU.add).then_inc(sems[f"{name}_sum_done"], 1)
                dve.wait_ge(sems[f"{name}_sum_done"], upto(f"{name}_sum_done", 0))
                shape = [P, src.shape[1], width]
                nc.vector.scalar_tensor_tensor(dst, sums.unsqueeze(2).broadcast_to(shape), -1.0 / width,
                                               src, ALU.mult, ALU.add).then_inc(sems[f"{name}_done"], 1)

            def centre_wv():
                dve.wait_ge(sems["wqkv_ps"], upto("wqkv_ps", 0))
                centre("wv", wqkv[:, 2 * D:3 * D].rearrange("p (h v) -> p h v", v=DH),
                       ps_c[:, 0:D].rearrange("p (h v) -> p h v", v=DH), wv_sum[:, :], DH)

            def centre_wo():
                dve.wait_ge(sems["ld_wo"], upto("ld_wo", 0))
                rows = wo[:, :].rearrange("p (a d) -> p a d", a=1)
                centre("wo", rows, rows, wo_sum[:, :], D)

            def centre_down():
                dve.wait_ge(sems["shared_hi"], upto("shared_hi", 0))
                dve.wait_ge(sems["ld_down"], upto("ld_down", 0))
                rows = w_down[:, :].rearrange("p (k d) -> p k d", d=D)
                centre("down", rows, rows, down_sum[:, :], D)

            def shared_low():
                dve.wait_ge(sems["shared_hi"], upto("shared_hi", 0))
                for n, w in enumerate((w_gate, w_up)):
                    tt(w[1][:, PAIRS * P:], ps_u[:, tb(n)], w[0][:, PAIRS * P:].bitcast(fp32), ALU.subtract)
                tt(w_rout[1][:, :], ps_u[:, 3 * P:4 * P], w_rout[0][:, :].bitcast(fp32),
                   ALU.subtract).then_inc(sems["shared_lo"], 1)

            def carry_wait():
                nc.vector.memset(carrier[:, :], 0.0)

            def stats(g, st, mv, sem_st, sem_mv, src):
                for t in range(T):
                    i = nc.vector.bn_stats(st[:, t, :], src(t))
                i.then_inc(sems[sem_st], 1)
                dve.wait_ge(sems[sem_st], upto(sem_st, g))
                carry_wait()
                for t in range(T):
                    i = nc.vector.bn_aggr(mv[:, t, :], st[:, t, :])
                i.then_inc(sems[sem_mv], 1)

            def rotate(b):
                def op(g, q):
                    if isinstance(g, int) and g == 0:
                        dve.wait_ge(sems["ld_cst"], upto("ld_cst", 0))
                    dve.wait_ge(sems["qkv_sb"], upto("qkv_sb", g, b + 1))
                    if due(c := upto("qk_done", g, b)):
                        dve.wait_ge(sems["qk_done"], c)
                    for r in range(R):
                        tt(pairs(rb[:, r, :]), pairs(qkv[q][:, b, r, 0:2 * D])[:, :, ::-1],
                           pairs(rot_s[:, r, :]), ALU.mult)
                    tt(ra[:, :, :], qkv[q][:, b, :, 0:2 * D], rot_c, ALU.mult).then_inc(sems["rot_ab"], 1)
                    dve.wait_ge(sems["rot_ab"], upto("rot_ab", g, b + 1))
                    if due(c := upto("kv_ab", g - 2, b + 1)):
                        dve.wait_ge(sems["kv_ab"], c)
                    if due(c := upto("qs_done", g - 2, b + 1)):
                        dve.wait_ge(sems["qs_done"], c)
                    tt(qk[q][:, b, :, :], ra[:, :, :], rb[:, :, :], ALU.add).then_inc(sems["qk_done"], 1)
                return op

            def near_dots(g, q):
                if due(c := upto("dots_done", g - 1)):
                    dve.wait_ge(sems["dots_done"], c)
                dve.wait_ge(sems["qk_done"], upto("qk_done", g))
                tt(dp[:, :, 0:R, :], qk[q][:, :, :, 0:D],
                   qk[q][:, :, 0, D:2 * D].unsqueeze(2).broadcast_to([P, NB, R, D]), ALU.mult)
                tt(dp[:, :, R, :], qk[q][:, :, 1, 0:D], qk[q][:, :, 1, D:2 * D], ALU.mult
                   ).then_inc(sems["dp_done"], 1)
                dve.wait_ge(sems["dp_done"], upto("dp_done", g))
                if due(c := upto("near_ab", g - 1)):
                    dve.wait_ge(sems["near_ab"], c)
                nc.vector.tensor_reduce(dots[:, :, :].rearrange("p n c -> p (n c)"),
                                        dp[:, :, :, :].rearrange("p n c (h u) -> p (n c h) u", u=DH),
                                        AX, ALU.add).then_inc(sems["dots_done"], 1)

            def outer_sum(b):
                def op(g, q):
                    dve.wait_ge(sems["kv_ab"], upto("kv_ab", g, b + 1))
                    if due(c := upto("pre_ps", g - 1, b + 1)):
                        dve.wait_ge(sems["pre_ps"], c)
                    tt(kv_w[b][:, :], kv_a[b][:, :], kv_b[b][:, :], ALU.add).then_inc(sems["kv_done"], 1)
                return op

            def apply_q(b):
                def op(g, q):
                    if due(c := upto("ret_done", g, b)):
                        dve.wait_ge(sems["ret_done"], c)
                    dve.wait_ge(sems["pre_ps"], upto("pre_ps", g, b + 1))
                    for r in range(R):
                        i = tt(qs[:, r, :].rearrange("p (n v) -> p n v", v=DH),
                               ps_s[:, :].rearrange("p (n v) -> p n v", v=DH),
                               qk[q][:, b, r, 0:D].unsqueeze(2).broadcast_to([P, D, DH]), ALU.mult)
                    i.then_inc(sems["qs_done"], 1)
                return op

            def sum_q(b):
                def op(g, q):
                    dve.wait_ge(sems["qs_done"], upto("qs_done", g, b + 1))
                    if due(c := upto("retf_done", g - 1)):
                        dve.wait_ge(sems["retf_done"], c)
                    for r in range(R):
                        i = nc.vector.tensor_reduce(ret[:, b, r, :].rearrange("p (h v) -> p h v", v=DH),
                                                    qs[:, r, :].rearrange("p (h u v) -> p h v u", u=DH, v=DH),
                                                    AX, ALU.add)
                    i.then_inc(sems["ret_done"], 1)
                return op

            heads = lambda a: a[:, :].rearrange("p (n v) -> p n v", v=DH)
            wide = lambda a: a[:, :].unsqueeze(2).broadcast_to([P, T * H, DH])

            def add_near(g, q):
                dve.wait_ge(sems["near_done"], upto("near_done", g))
                dve.wait_ge(sems["ret_done"], upto("ret_done", g))
                if due(c := upto("retn_done", g - 1)):
                    dve.wait_ge(sems["retn_done"], c)
                tt(ret_f[:, :], ret[:, :, :, :].rearrange("p n r d -> p (n r d)"),
                   near[:, :, :, :].rearrange("p n r d -> p (n r d)"), ALU.add).then_inc(sems["retf_done"], 1)

            def head_var(g, q):
                dve.wait_ge(sems["sq_done"], upto("sq_done", g))
                nc.vector.tensor_reduce(gn_v[:, :], heads(gn_sq), AX, ALU.add).then_inc(sems["gnv_done"], 1)

            def head_rstd(n):
                def op(g, q):
                    if n == 0:
                        dve.wait_ge(sems["gnv_done"], upto("gnv_done", g))
                        i = nc.vector.tensor_scalar(gn_t[:, :], gn_v[:, :], EPS, None, ALU.add)
                        i.then_inc(sems["gnr_done"], 1)
                        return
                    dve.wait_ge(sems["gnr_done"], upto("gnr_done", g, n))
                    if n == 1:
                        nc.vector.tensor_scalar(gn_h[:, :], gn_t[:, :], -0.5, None, ALU.mult)
                        i = nc.vector.tensor_scalar(gn_r[:, :].bitcast(i32), gn_t[:, :].bitcast(i32),
                                                    -0.5, float(0x5F3759DF), ALU.mult, ALU.add)
                    elif n % 3 == 2:
                        i = tt(gn_t[:, :], gn_r[:, :], gn_r[:, :], ALU.mult)
                    elif n % 3 == 0:
                        i = tt(gn_t[:, :], gn_t[:, :], gn_h[:, :], ALU.mult)
                    else:
                        i = nc.vector.scalar_tensor_tensor(gn_r[:, :], gn_t[:, :], 1.5, gn_r[:, :],
                                                           ALU.add, ALU.mult)
                    i.then_inc(sems["gnr_done"], 1)
                return op

            def scale_heads(g, q):
                dve.wait_ge(sems["gnr_done"], upto("gnr_done", g))
                if due(c := upto("rett_ps", g - 1)):
                    dve.wait_ge(sems["rett_ps"], c)
                tt(heads(ret_n), heads(ret_f), wide(gn_r), ALU.mult).then_inc(sems["retn_done"], 1)

            def stats_x1(g, q):
                dve.wait_ge(sems["x1_done"], upto("x1_done", g))
                stats(g, ln2_s, ln2_m, "ln2_st", "ln2_mv", lambda t: x1[q][:, t, :])

            def xm_low(g, q):
                dve.wait_ge(sems["xmhi_done"], upto("xmhi_done", g))
                if due(c := upto("up_ps", g - 2)):
                    dve.wait_ge(sems["up_ps"], c)
                tt(xm_lo[q][:, :], ps_a, xm_hi[q][:, :].bitcast(fp32), ALU.subtract
                   ).then_inc(sems["xmlo_done"], 1)

            def top_two(g, q):
                dve.wait_ge(sems["lg_ps"], upto("lg_ps", g))
                if isinstance(g, int) and g == 0:
                    dve.wait_ge(sems["ld_rbias"], upto("ld_rbias", 0))
                tt(lg[:, :, :], ps_a[:, 0:T * E].rearrange("p (t e) -> p t e", e=E),
                   rbias[:, :].unsqueeze(1).broadcast_to([P, T, E]), ALU.add).then_inc(sems["lg_sb"], 1)
                dve.wait_ge(sems["lg_sb"], upto("lg_sb", g))
                carry_wait()
                for t in range(T):
                    i = nc.vector.max(top[:, t, :], lg[:, t, :])
                i.then_inc(sems["top_done"], 1)
                dve.wait_ge(sems["top_done"], upto("top_done", g))
                tt(gap[:, :], top[:, :, 1], top[:, :, 0], ALU.subtract).then_inc(sems["gap_done"], 1)
                for t in range(T):
                    i = nc.vector.max_index(idx[:, t, :], top[:, t, :], lg[:, t, :])
                i.then_inc(sems["idx_done"], 1)
                dve.wait_ge(sems["idx_done"], upto("idx_done", g))
                nc.vector.tensor_copy(idx_f[:, :, :], idx[:, :, 0:2]).then_inc(sems["idxf_done"], 1)
                dve.wait_ge(sems["idxf_done"], upto("idxf_done", g))
                if due(c := upto("hotp_done", g - 1)):
                    dve.wait_ge(sems["hotp_done"], c)
                if isinstance(g, int) and g == 0:
                    dve.wait_ge(sems["stored"], AHEAD["stored"])
                tt(hot[:, :, :, :].rearrange("p t c e -> p (t c) e"),
                   count.unsqueeze(1).broadcast_to([P, 2 * T, E]),
                   idx_f[:, :, :].rearrange("p t c -> p (t c)").unsqueeze(2).broadcast_to([P, 2 * T, E]),
                   ALU.is_equal).then_inc(sems["hot_done"], 1)

            def hidden(k):
                def op(g, q):
                    dve.wait_ge(sems["up_ps"], upto("up_ps", g, k + 1))
                    if k < PAIRS:
                        dve.wait_ge(sems["silc_done"], upto("silc_done", g, k + 1))
                    else:
                        dve.wait_ge(sems["sil_done"], upto("sil_done", g, k + 1))
                    if due(c := upto("down_ps", g, k - 1)):
                        dve.wait_ge(sems["down_ps"], c)
                    other = silc[k % 2] if k < PAIRS else sil[(k + q) % 2]
                    tt(hid[(k + q) % 2][:, :], ps_u[:, :], other[:, :], ALU.mult).then_inc(sems["hid_done"], 1)
                return op

            run(dve, [
                (AT["centre_wv"], once(centre_wv)), (AT["shared_low"], once(shared_low)),
                (AT["centre_wo"], once(centre_wo)), (AT["centre_down"], once(centre_down)),
                *[(AT["rotate"][b], rotate(b)) for b in range(NB)],
                (AT["near_dots"], near_dots),
                *[(AT["outer_sum"][b], outer_sum(b)) for b in range(NB)],
                *[(AT["apply_q"][b], apply_q(b)) for b in range(NB)],
                *[(AT["sum_q"][b], sum_q(b)) for b in range(NB)],
                (AT["add_near"], add_near),
                (AT["head_var"], head_var),
                *[(AT["head_rstd"][0] + AT["head_rstd"][1] * n, head_rstd(n)) for n in range(RSQ)],
                (AT["scale_heads"], scale_heads),
                (AT["stats_x1"], stats_x1), (AT["xm_low"], xm_low),
                (AT["top_two"], top_two),
                *[(AT["hidden"] + k, hidden(k)) for k in range(UNITS)],
            ])

        @block.tensor
        def _(pe):
            mm = nc.tensor.matmul

            def transposes(dst, src):
                for t in range(T):
                    i = nc.tensor.transpose(dst[:, tb(t)], src(t), ident)
                return i

            def turn_wqkv():
                pe.wait_ge(sems["ld_ident"], upto("ld_ident", 0))
                for i, n in enumerate(("wq", "wk", "wv")):
                    pe.wait_ge(sems[f"ld_{n}"], upto(f"ld_{n}", 0))
                    t_ = nc.tensor.transpose(ps_g[:, tb(i)] if i < 2 else ps_c[:, 0:P], w_in[:, i, :], ident)
                    if i < 2:
                        ahead = ("up_ps", "c_ps")[i]
                        t_.then_inc(sems[ahead], AHEAD[ahead])
                t_.then_inc(sems["wqkv_ps"], 1)

            def turn_shared():
                for i, n in enumerate(("shg", "shu", "shd", "rout")):
                    pe.wait_ge(sems[f"ld_{n}"], upto(f"ld_{n}", 0))
                    t_ = nc.tensor.transpose(ps_u[:, tb(i)], w_in[:, 3 + i, :], ident)
                t_.then_inc(sems["shared_ps"], 1)

            def split_product(dst, w, cols, q):
                mm(dst, w[1][:, cols], xm_hi[q][:, :], start=True, stop=False)
                mm(dst, w[0][:, cols], xm_lo[q][:, :], start=False, stop=False)
                return mm(dst, w[0][:, cols], xm_hi[q][:, :], start=False, stop=True)

            def turn_xn(g, q):
                pe.wait_ge(sems["xn_done"], upto("xn_done", g))
                if last := reader("a", AT["turn_xn"], g):
                    pe.wait_ge(sems[last[0]], last[1])
                transposes(ps_a, lambda t: xn[:, t, :]).then_inc(sems["xnt_ps"], 1)

            def project(b):
                def op(g, q):
                    if isinstance(g, int) and g == 0 and b == 0:
                        pe.wait_ge(sems["wqk_sb"], upto("wqk_sb", 0))
                        pe.wait_ge(sems["wv_done"], upto("wv_done", 0))
                    pe.wait_ge(sems["xnt_sb"], upto("xnt_sb", g))
                    if last := reader("a", AT["project"][b], g):
                        pe.wait_ge(sems[last[0]], last[1])
                    if last := reader("b", AT["project"][b], g):
                        pe.wait_ge(sems[last[0]], last[1])
                    for r in range(R):
                        i = mm(ps_ab[:, 512 * r:512 * r + 3 * D], xn_t[:, tb(b * R + r)], wqkv[:, :],
                               start=True, stop=True)
                    i.then_inc(sems["proj_ps"], 1)
                return op

            def prefix(b):
                def op(g, q):
                    pe.wait_ge(sems["kv_done"], upto("kv_done", g, b + 1))
                    if last := reader("s0", AT["prefix"][b], g):
                        pe.wait_ge(sems[last[0]], last[1])
                    if last := reader("s1", AT["prefix"][b], g):
                        pe.wait_ge(sems[last[0]], last[1])
                    for c in range(KV // 512):
                        i = mm(ps_s[:, 512 * c:512 * c + 512], before, kv_w[b][:, 512 * c:512 * c + 512],
                               start=True, stop=True)
                    i.then_inc(sems["pre_ps"], 1)
                return op

            def turn_ret(g, q):
                pe.wait_ge(sems["retn_done"], upto("retn_done", g))
                if last := reader("s0", AT["turn_ret"], g):
                    pe.wait_ge(sems[last[0]], last[1])
                transposes(ps_s0, lambda t: ret_n[:, tb(t)]).then_inc(sems["rett_ps"], 1)

            def project_out(g, q):
                if isinstance(g, int) and g == 0:
                    pe.wait_ge(sems["wo_done"], upto("wo_done", 0))
                pe.wait_ge(sems["rett_sb"], upto("rett_sb", g))
                if last := reader("b", AT["project_out"], g):
                    pe.wait_ge(sems[last[0]], last[1])
                for t in range(T):
                    i = mm(ps_b[:, tb(t)], ret_t[:, tb(t)], wo[:, :], start=True, stop=True)
                i.then_inc(sems["wo_ps"], 1)

            def turn_xm(g, q):
                pe.wait_ge(sems["xm_done"], upto("xm_done", g))
                if last := reader("a", AT["turn_xm"], g):
                    pe.wait_ge(sems[last[0]], last[1])
                transposes(ps_a, lambda t: xm[:, t, :]).then_inc(sems["xmt_ps"], 1)

            def route(g, q):
                if isinstance(g, int) and g == 0:
                    pe.wait_ge(sems["shared_lo"], upto("shared_lo", 0))
                pe.wait_ge(sems["xmlo_done"], upto("xmlo_done", g))
                if last := reader("a", AT["route"], g):
                    pe.wait_ge(sems[last[0]], last[1])
                for t in range(T):
                    dst, hi, lo = ps_a[:, t * E:t * E + E], xm_hi[q][:, tb(t)], xm_lo[q][:, tb(t)]
                    mm(dst, hi, w_rout[1][:, 0:E], start=True, stop=False)
                    mm(dst, hi, w_rout[0][:, 0:E], start=False, stop=False)
                    i = mm(dst, lo, w_rout[0][:, 0:E], start=False, stop=True)
                i.then_inc(sems["lg_ps"], 1)

            def turn_comb(g, q):
                pe.wait_ge(sems["clo_done"], upto("clo_done", g))
                if last := reader("b", AT["turn_comb"], g):
                    pe.wait_ge(sems[last[0]], last[1])
                for t in range(T):
                    i = nc.tensor.transpose(ps_b[0:2 * E, tb(t)], comb_2[:, t, :].bitcast(fp32), ident)
                i.then_inc(sems["ct_ps"], 1)

            def spread(k):
                def op(g, q):
                    if k == 0:
                        if isinstance(g, int) and g == 0:
                            pe.wait_ge(sems["sel_done"], upto("sel_done", 0))
                        pe.wait_ge(sems["ct_sb"], upto("ct_sb", g))
                    if due(c := upto("cbc_done", g, k)):
                        pe.wait_ge(sems["cbc_done"], c)
                    mm(ps_c[:, :], sel[:, tb(k)], comb_t[q][:, :], start=True,
                       stop=True).then_inc(sems["c_ps"], 1)
                return op

            def gate(k):
                def op(g, q):
                    if isinstance(g, int) and g == 0 and k == 0:
                        pe.wait_ge(sems["wqk_sb"], upto("wqk_sb", 0))
                        pe.wait_ge(sems["gate_lo"], upto("gate_lo", 0))
                    if due(c := upto("sil_done", g, k)):
                        pe.wait_ge(sems["sil_done"], c)
                    split_product(ps_g[:, :], w_gate, tb(k), q).then_inc(sems["gate_ps"], 1)
                return op

            def up(k):
                def op(g, q):
                    if isinstance(g, int) and g == 0 and k == 0:
                        pe.wait_ge(sems["shared_lo"], upto("shared_lo", 0))
                        pe.wait_ge(sems["up_lo"], upto("up_lo", 0))
                    if due(c := upto("hid_done", g, k)):
                        pe.wait_ge(sems["hid_done"], c)
                    split_product(ps_u[:, :], w_up, tb(k), q).then_inc(sems["up_ps"], 1)
                return op

            def down(k):
                def op(g, q):
                    pe.wait_ge(sems["hid_done"], upto("hid_done", g, k + 1))
                    if isinstance(g, int) and g == 0 and k == 0:
                        pe.wait_ge(sems["down_done"], upto("down_done", 0))
                    if k == 0:
                        if due(c := upto("y2_sb", g - 1)):
                            pe.wait_ge(sems["y2_sb"], c)
                    for t in range(T):
                        i = mm(ps_y[:, tb(t)], hid[(k + q) % 2][:, tb(t)], w_down[:, k * D:k * D + D],
                               start=(k == 0 and t == 0), stop=(k == UNITS - 1 and t == T - 1))
                    i.then_inc(sems["down_ps"], 1)
                return op

            run(pe, [
                (AT["turn_wqkv"], once(turn_wqkv)), (AT["turn_shared"], once(turn_shared)),
                (AT["turn_xn"], turn_xn),
                *[(AT["project"][b], project(b)) for b in range(NB)],
                *[(AT["prefix"][b], prefix(b)) for b in range(NB)],
                (AT["turn_ret"], turn_ret), (AT["project_out"], project_out), (AT["turn_xm"], turn_xm),
                (AT["route"], route), (AT["turn_comb"], turn_comb),
                *[(AT["spread"] + k, spread(k)) for k in range(PAIRS)],
                *[(AT["gate"] + k, gate(k)) for k in range(UNITS)],
                *[(AT["up"] + k, up(k)) for k in range(UNITS)],
                *[(AT["down"] + k, down(k)) for k in range(UNITS)],
            ])


_INS = ['L0_attn_x', 'L0_attn_WQ', 'L0_attn_WK', 'L0_attn_WV', 'L0_attn_WO', 'L0_attn_gamma',
        'L0_attn_beta', 'L0_ffn_router_w', 'L0_ffn_router_bias', 'L0_ffn_up_proj', 'L0_ffn_gate_proj',
        'L0_ffn_down_proj', 'L0_ffn_sh_gate', 'L0_ffn_sh_up', 'L0_ffn_sh_down']


def kernel(**inputs):
    import concourse.bacc as _bacc
    from concourse.bass_utils import run_bass_kernel_spmd as _run

    nc = _bacc.Bacc("TRN2", target_bir_lowering=False, num_devices=1)
    arrays, args = {}, []
    for name in _INS:
        a = np.ascontiguousarray(inputs[name])
        arrays[f"in_{name}"] = a
        args.append(nc.dram_tensor(f"in_{name}", a.shape, mybir.dt.from_np(a.dtype), kind="ExternalInput").ap())
    table = constants()
    arrays["tables"] = table
    args.append(nc.dram_tensor("tables", table.shape, mybir.dt.float32, kind="ExternalInput").ap())
    args.append(nc.dram_tensor("out_0", (B, S, D), mybir.dt.float32, kind="ExternalOutput").ap())
    build(nc, *args)
    r = _run(nc, [arrays], core_ids=[0])
    return r.results[0]["out_0"]
```
